# Optimizing a Trainium2 kernel written in Bass

```python
import numpy as np
import jax
import jax.numpy as jnp

def _softmax(x, axis=-1):
    return jax.nn.softmax(x, axis=axis)

def _gelu(x):
    return jax.nn.gelu(x, approximate=True)

def _silu(x):
    return jax.nn.silu(x)

def _sigmoid(x):
    return jax.nn.sigmoid(x)

def _layernorm(x, axis=-1, eps=1e-05):
    m = jnp.mean(x, axis=axis, keepdims=True)
    v = jnp.var(x, axis=axis, keepdims=True)
    return (x - m) / jnp.sqrt(v + eps)

def _scatter_add(tgt, idx, src, axis=0):
    return tgt.at[idx].add(src)

def _segment_sum(src, seg, n):
    return jax.ops.segment_sum(src, seg, n)
kernel_name = 'mk_conv_seq_d2_conv_nchw512_r2_0c22c0'

def setup_inputs(seed: int=0):
    np.random.seed(seed)
    _w = jnp.asarray

    def _rec_inputs():
        import jax
        import jax.numpy as jnp
        _gk = jax.random.key(seed)
        x = 7.22e-05 + 1 * jax.random.normal(jax.random.fold_in(_gk, 1), (4, 256, 32, 32), jnp.float32)
        return x
    x = _rec_inputs()

    def _L0_conv_setup():
        import jax, jax.numpy as jnp
        import numpy as np
        B_, C_, H_, W_ = (4, 256, 32, 32)
        key = jax.random.key(seed)
        kx, kb, kc, kd, kg = jax.random.split(key, 5)
        scale = 1.0 / np.sqrt(C_)
        x = jax.random.normal(kx, (B_, C_, H_, W_), dtype=jnp.float32)
        Wb = jax.random.normal(kb, (C_, C_), dtype=jnp.float32) * scale
        Wc = jax.random.normal(kc, (C_, C_), dtype=jnp.float32) * scale
        Wd = jax.random.normal(kd, (C_, C_), dtype=jnp.float32) * scale
        gamma = jax.random.normal(kg, (1,), dtype=jnp.float32) * 0.1
        return {'x': x, 'Wb': Wb, 'Wc': Wc, 'Wd': Wd, 'gamma': gamma}
    _L0_conv_all = _L0_conv_setup()
    _L0_conv_in = {k: v for k, v in _L0_conv_all.items() if k in ('Wb', 'Wc', 'Wd', 'gamma')}
    del _L0_conv_all

    def _L1_conv_setup():
        import jax, jax.numpy as jnp
        import numpy as np
        C = 256
        NH = 4
        HD = C // NH
        G = 32
        EPS = 1e-05

        def _group_norm(x, gamma, beta):
            b, c, h, w = x.shape
            xr = x.reshape(b, G, c // G, h, w)
            mean = xr.mean(axis=(2, 3, 4), keepdims=True)
            var = xr.var(axis=(2, 3, 4), keepdims=True)
            xn = ((xr - mean) * jax.lax.rsqrt(var + EPS)).reshape(b, c, h, w)
            return xn * gamma[None, :, None, None] + beta[None, :, None, None]

        def _conv1x1(x, w, b):
            return jnp.einsum('oc,bchw->bohw', w, x) + b[None, :, None, None]
        key = jax.random.key(seed)
        ks = jax.random.split(key, 11)
        s = 1.0 / np.sqrt(C)
        return {'x': jax.random.normal(ks[0], (16, C, 32, 32), dtype=jnp.float32), 'gamma': jnp.ones((C,), jnp.float32), 'beta': jnp.zeros((C,), jnp.float32), 'wq': jax.random.normal(ks[1], (C, C), jnp.float32) * s, 'bq': jax.random.normal(ks[2], (C,), jnp.float32) * 0.01, 'wk': jax.random.normal(ks[3], (C, C), jnp.float32) * s, 'bk': jax.random.normal(ks[4], (C,), jnp.float32) * 0.01, 'wv': jax.random.normal(ks[5], (C, C), jnp.float32) * s, 'bv': jax.random.normal(ks[6], (C,), jnp.float32) * 0.01, 'wp': jax.random.normal(ks[7], (C, C), jnp.float32) * s, 'bp': jax.random.normal(ks[8], (C,), jnp.float32) * 0.01}
    _L1_conv_all = _L1_conv_setup()
    _L1_conv_in = {k: v for k, v in _L1_conv_all.items() if k in ('gamma', 'beta', 'wq', 'bq', 'wk', 'bk', 'wv', 'bv', 'wp', 'bp')}
    del _L1_conv_all
    return {'x': x, 'L0_conv_Wb': _L0_conv_in['Wb'], 'L0_conv_Wc': _L0_conv_in['Wc'], 'L0_conv_Wd': _L0_conv_in['Wd'], 'L0_conv_gamma': _L0_conv_in['gamma'], 'L1_conv_gamma': _L1_conv_in['gamma'], 'L1_conv_beta': _L1_conv_in['beta'], 'L1_conv_wq': _L1_conv_in['wq'], 'L1_conv_bq': _L1_conv_in['bq'], 'L1_conv_wk': _L1_conv_in['wk'], 'L1_conv_bk': _L1_conv_in['bk'], 'L1_conv_wv': _L1_conv_in['wv'], 'L1_conv_bv': _L1_conv_in['bv'], 'L1_conv_wp': _L1_conv_in['wp'], 'L1_conv_bp': _L1_conv_in['bp']}

def reference(x, L0_conv_Wb, L0_conv_Wc, L0_conv_Wd, L0_conv_gamma, L1_conv_gamma, L1_conv_beta, L1_conv_wq, L1_conv_bq, L1_conv_wk, L1_conv_bk, L1_conv_wv, L1_conv_bv, L1_conv_wp, L1_conv_bp):
    import jax
    import jax.numpy as jnp

    def _L0_conv_ref(x, Wb, Wc, Wd, gamma):
        import jax, jax.numpy as jnp
        import numpy as np
        B_, C_, H_, W_ = (4, 256, 32, 32)
        b, c, h, w = x.shape
        n = h * w
        xf = x.reshape(b, c, n)
        Bm = jnp.einsum('oc,bcn->bon', Wb, xf)
        Cm = jnp.einsum('oc,bcn->bon', Wc, xf)
        Dm = jnp.einsum('oc,bcn->bon', Wd, xf)
        S = jax.nn.softmax(jnp.einsum('bcn,bcm->bnm', Bm, Cm), axis=-1)
        att = jnp.einsum('bcm,bnm->bcn', Dm, S).reshape(b, c, h, w)
        return gamma * att + x

    def _L1_conv_ref(x, gamma, beta, wq, bq, wk, bk, wv, bv, wp, bp):
        import jax, jax.numpy as jnp
        import numpy as np
        C = 256
        NH = 4
        HD = C // NH
        G = 32
        EPS = 1e-05

        def _group_norm(x, gamma, beta):
            b, c, h, w = x.shape
            xr = x.reshape(b, G, c // G, h, w)
            mean = xr.mean(axis=(2, 3, 4), keepdims=True)
            var = xr.var(axis=(2, 3, 4), keepdims=True)
            xn = ((xr - mean) * jax.lax.rsqrt(var + EPS)).reshape(b, c, h, w)
            return xn * gamma[None, :, None, None] + beta[None, :, None, None]

        def _conv1x1(x, w, b):
            return jnp.einsum('oc,bchw->bohw', w, x) + b[None, :, None, None]
        b, c, h, w = x.shape
        hw = h * w
        scale = HD ** (-0.5)
        hn = _group_norm(x, gamma, beta)
        q = _conv1x1(hn, wq, bq).reshape(b, NH, HD, hw)
        k = _conv1x1(hn, wk, bk).reshape(b, NH, HD, hw)
        v = _conv1x1(hn, wv, bv).reshape(b, NH, HD, hw)
        attn = jnp.einsum('bhdq,bhdk->bhqk', q, k) * scale
        attn = jax.nn.softmax(attn, axis=-1)
        out = jnp.einsum('bhqk,bhdk->bhdq', attn, v)
        out = out.reshape(b, c, h, w)
        out = _conv1x1(out, wp, bp)
        return x + out

    def _gn(v, G=32, eps=1e-05):
        B_, C_, H_, W_ = v.shape
        g = v.reshape(B_, G, C_ // G, H_, W_)
        m = jnp.mean(g, axis=(2, 3, 4), keepdims=True)
        s = jnp.var(g, axis=(2, 3, 4), keepdims=True)
        return ((g - m) / jnp.sqrt(s + eps)).reshape(v.shape)

    def _ln_c(v, eps=1e-06):
        m = jnp.mean(v, axis=1, keepdims=True)
        s = jnp.var(v, axis=1, keepdims=True)
        return (v - m) / jnp.sqrt(s + eps)

    def _ln_t(v, eps=1e-05):
        m = jnp.mean(v, axis=-1, keepdims=True)
        s = jnp.var(v, axis=-1, keepdims=True)
        return (v - m) / jnp.sqrt(s + eps)

    def _to_tokens(v):
        B_, C_, H_, W_ = v.shape
        return v.reshape(B_, C_, H_ * W_).transpose(0, 2, 1)

    def _from_tokens(t, like):
        B_, C_, H_, W_ = like.shape
        return t.transpose(0, 2, 1).reshape(B_, C_, H_, W_)
    x = _L0_conv_ref(x, L0_conv_Wb, L0_conv_Wc, L0_conv_Wd, L0_conv_gamma)
    x = _L1_conv_ref(x, L1_conv_gamma, L1_conv_beta, L1_conv_wq, L1_conv_bq, L1_conv_wk, L1_conv_bk, L1_conv_wv, L1_conv_bv, L1_conv_wp, L1_conv_bp)
    return x

_drawn_inputs = setup_inputs


def setup_inputs(seed=0):
    import zlib

    import numpy as np

    out = dict(_drawn_inputs(seed))
    spreads = {'L1_conv_gamma': (1.0, 0.2), 'L1_conv_beta': (0.0, 0.1)}
    factors = {'L1_conv_bq': 54.454, 'L1_conv_bk': 64.0, 'L1_conv_bv': 5.746, 'L1_conv_bp': 5.982}
    for name, (base, spread) in spreads.items():
        noise = np.random.default_rng([zlib.crc32(name.encode()), seed]).standard_normal(out[name].shape)
        drawn = base * np.exp(spread * noise) if base else spread * noise
        out[name] = jnp.asarray(drawn.astype(out[name].dtype))
    for name, factor in factors.items():
        out[name] = (out[name] * factor).astype(out[name].dtype)
    return out
```

```python
from contextlib import ExitStack

import concourse.bass as bass
from concourse import mybir

F32 = mybir.dt.float32
F32R = mybir.dt.float32r
ALU = mybir.AluOpType
ACT = mybir.ActivationFunctionType
AX_X = mybir.AxisListType.X

P = 128
IMAGES = 4
C = 256
KT = C // P
N = 1024
H = 512
NT = N // P
HEADS = 4
HD = C // HEADS
PAIRS = HEADS // 2
GROUP = C // 32
EPS = 1e-5
QSCALE = HD ** -0.5

T0_IMAGE = NT
T1_IMAGE = HEADS * NT
T1_BASE = IMAGES * T0_IMAGE
LAG = 2

G0_BASE = 2
G0_IMAGE = 12
G0_A, G0_AV, G0_OUT = 0, 4, 8
GN_BASE = G0_BASE + IMAGES * G0_IMAGE
G1_BASE = GN_BASE + 2
G1_IMAGE = 24
G1_PAIR0 = [0, 2, 4, 6]
G1_V = [1, 3, 5, 7]
G1_PAIR1 = [8, 9, 10, 11]
G1_AV = [12, 13, 14, 15, 16, 19, 20, 21]
G1_OUT = [17, 18, 22, 23]

EXP_CREDIT = 2
TRANS_CREDIT = 4
SPLIT_CREDIT = 2
GROUP_CREDIT = 6
EVAC_CREDIT = 2

GN_STEPS = [10, 15, 20, 25]
OUT_STEP = 25

FREE_CREDIT = 1

BQ, BK, BV, BP, GNW, GNB, GAMMA = 0, 2, 4, 6, 8, 10, 12
NVEC = 13
WEIGHTS = ["b", "c", "d", "q", "k", "v", "p"]


def products(his, los):
    (ah, bh), (al, bl) = his, los
    return [(ah, bh), (al, bh), (ah, bl)]


def build(nc, x, xT, weights, vecs, out):
    y_dram = nc.dram_tensor("y_scratch", (IMAGES, KT, P, N), F32, kind="Internal").ap()
    ctx = ExitStack()
    with ctx:
        def sb(name, shape, dt=F32, scope=ctx):
            return scope.enter_context(nc.sbuf_tensor(name, shape, dt))

        def sem(name):
            return ctx.enter_context(nc.semaphore(name))

        vec = sb("vec", [P, NVEC])
        bq8 = sb("bq8", [P, 2])
        ident = sb("ident", [P, P])
        gavg = sb("gavg", [P, P])
        gn_mv = sb("gn_mv", [P, IMAGES, KT, 2])
        gn_tmp = sb("gn_tmp", [P, 6, IMAGES, KT])
        gn_scale = sb("gn_scale", [P, IMAGES + 1, 2 * KT])
        gn_now = sb("gn_now", [P, 2 * KT])
        y_stats = sb("y_stats", [P, IMAGES * KT * 2 * 6])
        negmax = sb("negmax", [P, 2])
        rowsum = sb("rowsum", [P, 2])
        rsum = sb("rsum", [P, 2])
        w_hi = {w: sb(f"w{w}_hi", [P, KT, C], F32R) for w in "dqkvp"}
        w_lo = {w: sb(f"w{w}_lo", [P, KT, C], F32R) for w in "dqkvp"}
        start = ExitStack()
        w_raw = {w: sb(f"w{w}_raw", [P, KT, C], F32, start) for w in WEIGHTS}
        bc_hi = {w: sb(f"w{w}_hi", [P, KT, C], F32R, start) for w in "bc"}
        bc_lo = {w: sb(f"w{w}_lo", [P, KT, C], F32R, start) for w in "bc"}
        start.close()
        w_hi.update(bc_hi)
        w_lo.update(bc_lo)
        pt_hi = sb("pt_hi", [P, 2, NT, H], F32R)
        pt_lo = sb("pt_lo", [P, 2, NT, H], F32R)
        prob = sb("prob", [P, 2, N])

        layer0 = ExitStack()
        wk_hi = sb("wbc_hi", [P, KT, C], F32R, layer0)
        wk_lo = sb("wbc_lo", [P, KT, C], F32R, layer0)
        x_raw = sb("x_raw", [P, KT, N], F32, layer0)
        x_hi = sb("x_hi", [P, KT, N], F32R, layer0)
        x_lo = sb("x_lo", [P, KT, N], F32R, layer0)
        xT_raw = sb("xT_raw", [P, NT, C], F32, layer0)
        xT_hi = sb("xT_hi", [P, NT, C], F32R, layer0)
        xT_lo = sb("xT_lo", [P, NT, C], F32R, layer0)
        a_hi = sb("a_hi", [P, KT, N], F32R, layer0)
        a_lo = sb("a_lo", [P, KT, N], F32R, layer0)
        u_hi = sb("u_hi", [P, KT, N], F32R, layer0)
        u_lo = sb("u_lo", [P, KT, N], F32R, layer0)
        y_out = sb("y_out", [P, 4, H], F32, layer0)
        layer0.close()

        h_hi = sb("h_hi", [P, KT, N], F32R)
        h_lo = sb("h_lo", [P, KT, N], F32R)
        q_st = sb("q_st", [P, HEADS, N], F32R)
        k_st = sb("k_st", [P, 2, HEADS, N], F32R)
        v_st = sb("v_st", [P, NT, HEADS, 2, HD], F32R)
        qk_hi = sb("qk_hi", [P, 2, H], F32R)
        qk_lo = sb("qk_lo", [P, 2, H], F32R)
        o_sum = sb("o_sum", [P, 2, H])
        o_hi = sb("o_hi", [P, KT, H], F32R)
        o_lo = sb("o_lo", [P, KT, H], F32R)
        y_in = sb("y_in", [P, KT, 2, H])
        y_res = sb("y_res", [P, 2, H])

        scores = ctx.enter_context(nc.psum_tensor("scores", [P, 2, N], F32))
        trans = ctx.enter_context(nc.psum_tensor("trans", [P, 2, H], F32))
        acc = ctx.enter_context(nc.psum_tensor("acc", [P, 2, H], F32))

        consts_ready = sem("consts_ready")
        vec_loaded = sem("vec_loaded")
        w_loaded = sem("w_loaded")
        w_high = sem("w_high")
        w_split = sem("w_split")
        x_loaded = sem("x_loaded")
        x_high = sem("x_high")
        x_split = sem("x_split")
        xT_loaded = sem("xT_loaded")
        xT_high = sem("xT_high")
        xT_split = sem("xT_split")
        res_loaded = sem("res_loaded")
        y_summed = sem("y_summed")
        y_ready = sem("y_ready")
        y_stored = sem("y_stored")
        scores_ready = sem("scores_ready")
        max_ready = sem("max_ready")
        exp_ready = sem("exp_ready")
        rsum_ready = sem("rsum_ready")
        prob_ready = sem("prob_ready")
        transposed = sem("transposed")
        pt_high = sem("pt_high")
        pt_split = sem("pt_split")
        acc_done = sem("acc_done")
        acc_high = sem("acc_high")
        acc_evac = sem("acc_evac")
        gn_chain = sem("gn_chain")
        gn_var = sem("gn_var")
        gn_sqrt = sem("gn_sqrt")
        gn_stats = sem("gn_stats")
        gn_dev = sem("gn_dev")
        gn_affine = sem("gn_affine")
        y_loaded = sem("y_loaded")
        h_full = sem("h_full")
        h_high = sem("h_high")
        h_split = sem("h_split")
        qk_stacked = [sem("qk_stacked0"), sem("qk_stacked1")]
        o_part = sem("o_part")
        o_high = sem("o_high")
        o_split = sem("o_split")
        yres_loaded = sem("yres_loaded")
        out_stored = sem("out_stored")
        pool_steps = sem("pool_steps")

        Q_DMA, K_DMA = 4 * 16, 8 * 16
        QK_IMAGE = PAIRS * (Q_DMA + K_DMA)

        def qk_dma_before(r):
            return (r // 4) * (Q_DMA + K_DMA) + (Q_DMA if r % 4 >= 2 else 0)

        def flat(ap):
            return ap.rearrange("p a b -> p (a b)")

        def pt_block(buf, half_slot, t, h):
            return buf[:, half_slot, 4 * h:4 * h + 4, (t % 4) * P:(t % 4 + 1) * P]

        def av1_after(s):
            return (s - 9) // 4 if s >= 9 and (s - 9) % 4 == 0 else None

        block = ctx.enter_context(nc.Block())

        @block.sync
        def _(sp):
            for s in (y_stored, out_stored, *qk_stacked):
                sp.sem_inc(s, FREE_CREDIT)
            sp.dma_start(vec[:, :], vecs).then_inc(vec_loaded, 16)
            for w in WEIGHTS[:2]:
                sp.dma_start(w_raw[w][:, :, :], weights[w].rearrange("(k p) c -> p k c", p=P)).then_inc(w_loaded, 16)
            sp.dma_start(x_raw[:, :, :], x[0].rearrange("k p n -> p k n")).then_inc(x_loaded, 16)
            sp.wait_ge(w_loaded, 2 * 16)
            for n, w in enumerate(WEIGHTS[2:]):
                sp.dma_start(w_raw[w][:, :, :], weights[w].rearrange("(k p) c -> p k c", p=P)).then_inc(w_loaded, 16)

            with sp.Fori(0, IMAGES) as i:
                sp.wait_ge(xT_split, FREE_CREDIT + i)
                sp.dma_start(xT_raw[:, :, :], xT[i].rearrange("(j p) c -> p j c", p=P)).then_inc(xT_loaded, 16)
                sp.wait_ge(y_stored, FREE_CREDIT + i * 64)
                for a in range(4):
                    sp.dma_start(y_out[:, a, :], x[i, a % 2, :, (a // 2) * H:(a // 2 + 1) * H]).then_inc(res_loaded, 16)
                sp.wait_ge(x_split, i + 1)
                sp.dma_start(x_raw[:, :, :], x[(i + 1) % IMAGES].rearrange("k p n -> p k n")).then_inc(x_loaded, 16)
                for a in range(4):
                    sp.wait_ge(y_ready, 4 * i + a + 1)
                    sp.dma_start(y_dram[i, a % 2, :, (a // 2) * H:(a // 2 + 1) * H], y_out[:, a, :]).then_inc(y_stored, 16)

            sp.wait_ge(y_stored, FREE_CREDIT + IMAGES * 64)
            sp.wait_ge(x_split, IMAGES + 1)
            sp.dma_start(y_in[:, :, :, :], y_dram[0].rearrange("k p (a n) -> p k a n", a=2)).then_inc(y_loaded, 16)

            def restack(i, r):
                pair, is_k, half, slot = r // 4, r % 4 >= 2, r % 2, r % 2
                cols = slice(half * H, (half + 1) * H)
                a = (G1_PAIR0 + G1_PAIR1)[r]
                sp.wait_ge(acc_evac, EVAC_CREDIT + G1_BASE + G1_IMAGE * i + a + 1)
                for n in range(2):
                    head, rows = 2 * pair + n, slice(n * HD, (n + 1) * HD)
                    for part, src in enumerate((qk_hi, qk_lo)):
                        if is_k:
                            dests = [k_st[u * HD:(u + 1) * HD, part, head, cols] for u in range(2)]
                        else:
                            dests = [q_st[part * HD:(part + 1) * HD, head, cols]]
                        for d in dests:
                            sp.dma_start(d.bitcast(F32), src[rows, slot, :].bitcast(F32)).then_inc(qk_stacked[slot], 16)

            def load_residual(i, half):
                sp.wait_ge(out_stored, FREE_CREDIT + 64 * i + 32 * half)
                for o in range(2):
                    sp.dma_start(y_res[:, o, :], y_dram[i, o, :, half * H:(half + 1) * H]).then_inc(yres_loaded, 16)

            def store(i, half):
                for o in range(2):
                    sp.wait_ge(acc_evac, EVAC_CREDIT + G1_BASE + G1_IMAGE * i + G1_OUT[2 * half + o] + 1)
                    sp.dma_start(out[i, o, :, half * H:(half + 1) * H], y_res[:, o, :]).then_inc(out_stored, 16)

            with sp.Fori(0, IMAGES) as i:
                for r in range(4):
                    restack(i, r)
                load_residual(i, 0)
                for r in range(4, 8):
                    restack(i, r)
                sp.wait_ge(h_split, 4 * i + 4)
                sp.dma_start(y_in[:, :, :, :], y_dram[(i + 1) % IMAGES].rearrange("k p (a n) -> p k a n", a=2)).then_inc(y_loaded, 16)
                store(i, 0)
                load_residual(i, 1)
                store(i, 1)
            sp.wait_ge(out_stored, FREE_CREDIT + IMAGES * 64)
            sp.wait_ge(y_loaded, (IMAGES + 1) * 16)

        @block.gpsimd
        def _(pool):
            pool.sem_inc(o_split, FREE_CREDIT)
            nc.gpsimd.memset(ident[:, :], 0.0).then_inc(consts_ready, 1)
            nc.gpsimd.memset(gavg[:, :], 1.0 / GROUP).then_inc(consts_ready, 1)
            pool.wait_ge(consts_ready, 2)
            nc.gpsimd.affine_select(out=ident[:, :], in_=ident[:, :], compare_op=ALU.not_equal, fill=1.0,
                                    base=0, pattern=[[-1, P]], channel_multiplier=1).then_inc(consts_ready, 1)
            groups = gavg[:, :].rearrange("p (g c) -> p g c", c=GROUP)
            nc.gpsimd.affine_select(out=groups, in_=groups, compare_op=ALU.is_ge, fill=0.0, base=0,
                                    pattern=[[-GROUP, P // GROUP], [0, GROUP]], channel_multiplier=1).then_inc(consts_ready, 1)
            pool.wait_ge(consts_ready, 4)
            nc.gpsimd.affine_select(out=groups, in_=groups, compare_op=ALU.is_ge, fill=0.0, base=GROUP - 1,
                                    pattern=[[GROUP, P // GROUP], [0, GROUP]], channel_multiplier=-1).then_inc(consts_ready, 1)

            def wait_scalar(semaphore, value):
                pool.wait_ge(semaphore, value)
                pool.sem_inc(pool_steps, 1)

            def normalise(t0, t):
                wait_scalar(rsum_ready, t0 + t + 1)
                p = prob[:, t % 2, :]
                nc.gpsimd.tensor_scalar(p, p, rsum[:, t % 2:t % 2 + 1], 1.0, ALU.mult, ALU.mult)\
                    .then_inc(prob_ready, 1)

            def norm_chunk(n, c):
                k, half = c // 2, c % 2
                if c == 0:
                    wait_scalar(y_loaded, 16 * n + 16)
                    wait_scalar(gn_affine, n + 1)
                y = y_in[:, k, half, :]
                nc.gpsimd.tensor_scalar(y, y, gn_now[:, k:k + 1], gn_now[:, KT + k:KT + k + 1],
                                        ALU.mult, ALU.add).then_inc(h_full, 1)

            def norm_chunk_low(n, c):
                k, half = c // 2, c % 2
                pool.wait_ge(h_high, 4 * n + c + 1)
                dst = slice(half * H, (half + 1) * H)
                nc.gpsimd.tensor_tensor(h_lo[:, k, dst], y_in[:, k, half, :], h_hi[:, k, dst].bitcast(F32),
                                        ALU.subtract).then_inc(h_split, 1)

            with pool.Fori(0, IMAGES) as i:
                for t in range(T0_IMAGE):
                    normalise(T0_IMAGE * i, t)

            for c in range(4):
                norm_chunk(0, c)
            for c in range(4):
                norm_chunk_low(0, c)

            with pool.Fori(0, IMAGES) as i:
                for s in range(T1_IMAGE + LAG + 1):
                    if s < T1_IMAGE:
                        normalise(T1_BASE + T1_IMAGE * i, s)
                    if s in GN_STEPS:
                        norm_chunk(i + 1, GN_STEPS.index(s))
                    if s - 2 in GN_STEPS:
                        norm_chunk_low(i + 1, GN_STEPS.index(s - 2))
                    j = av1_after(s) if s < T1_IMAGE + LAG else 7
                    if j is not None and j % 2:
                        pool.wait_ge(o_high, 4 * i + j // 2 + 1)
                        pair = (j // 2) % 2
                        nc.gpsimd.tensor_tensor(o_lo[:, pair, :], o_sum[:, (j // 2) % 2, :],
                                                o_hi[:, pair, :].bitcast(F32), ALU.subtract).then_inc(o_split, 1)

        @block.scalar
        def _(act):
            act.sem_inc(exp_ready, EXP_CREDIT)

            def acc_bank(a):
                return acc[:, a % 2, :]

            def wait_acc(g0, a):
                act.wait_ge(acc_done, GROUP_CREDIT + g0 + a + 1)

            def exp(t0, t):
                act.wait_ge(max_ready, t0 + t + 1)
                act.wait_ge(transposed, TRANS_CREDIT + 2 * (t0 + t) - 2)
                nc.scalar.activation(prob[:, t % 2, :], scores[:, t % 2, :], ACT.Exp,
                                     bias=negmax[:, t % 2:t % 2 + 1], scale=1.0,
                                     accum_out=rowsum[:, t % 2:t % 2 + 1]).then_inc(exp_ready, 1)

            def trans_high(t0, t, av_before):
                if t % 4 == 0:
                    act.wait_ge(acc_done, GROUP_CREDIT + av_before + 1)
                for h in range(2):
                    act.wait_ge(transposed, TRANS_CREDIT + 2 * (t0 + t) + h + 1)
                    nc.scalar.activation(pt_block(pt_hi, (t // 4) % 2, t, h),
                                         trans[:, h, :].rearrange("p (j n) -> p j n", n=P),
                                         ACT.Copy).then_inc(pt_high, 1)

            act.wait_ge(w_loaded, 2 * 16)
            for n, w in enumerate(WEIGHTS):
                if n == 2:
                    act.wait_ge(x_loaded, 16)
                    nc.scalar.activation(flat(x_hi), flat(x_raw), ACT.Copy).then_inc(x_high, 1)
                    act.wait_ge(w_loaded, len(WEIGHTS) * 16)
                nc.scalar.activation(flat(w_hi[w]), flat(w_raw[w]), ACT.Copy,
                                     scale=QSCALE if w == "q" else 1.0).then_inc(w_high, 1)
            for ct in range(KT):
                wait_acc(0, ct)
                nc.scalar.activation(wk_hi[:, ct, :], acc[:, ct, 0:C], ACT.Copy).then_inc(acc_high, 1)

            with act.Fori(0, IMAGES) as i:
                g0, t0 = G0_BASE + G0_IMAGE * i, T0_IMAGE * i
                for a in range(4):
                    half, ct = a // 2, a % 2
                    wait_acc(g0, G0_A + a)
                    nc.scalar.activation(a_hi[:, ct, half * H:(half + 1) * H], acc_bank(a), ACT.Copy)\
                        .then_inc(acc_high, 1)
                for s in range(T0_IMAGE + LAG):
                    if s >= LAG:
                        t = s - LAG
                        trans_high(t0, t, g0 - G0_IMAGE + G0_AV + 2 * (t // 4) + 1)
                    if s < T0_IMAGE:
                        exp(t0, s)
                    if s == 2:
                        act.wait_ge(xT_loaded, 16 * i + 16)
                        nc.scalar.activation(flat(xT_hi), flat(xT_raw), ACT.Copy).then_inc(xT_high, 1)
                    if s == T0_IMAGE - 1:
                        act.wait_ge(x_loaded, 16 * i + 32)
                        nc.scalar.activation(flat(x_hi), flat(x_raw), ACT.Copy).then_inc(x_high, 1)
                for n in range(4):
                    half, ct = n // 2, n % 2
                    wait_acc(g0, G0_AV + n)
                    nc.scalar.activation(u_hi[:, ct, half * H:(half + 1) * H], acc_bank(n), ACT.Copy)\
                        .then_inc(acc_high, 1)

            act.wait_ge(gn_var, 1)
            nc.scalar.activation(gn_tmp[:, 3, :, :], gn_tmp[:, 2, :, :], ACT.Sqrt).then_inc(gn_sqrt, 1)

            def norm_chunk_high(n, c):
                k, half = c // 2, c % 2
                act.wait_ge(h_full, 4 * n + c + 1)
                nc.scalar.activation(h_hi[:, k, half * H:(half + 1) * H], y_in[:, k, half, :], ACT.Copy)\
                    .then_inc(h_high, 1)

            for c in range(4):
                norm_chunk_high(0, c)

            with act.Fori(0, IMAGES) as i:
                g1, t1 = G1_BASE + G1_IMAGE * i, T1_BASE + T1_IMAGE * i

                def qk_high(r):
                    a = (G1_PAIR0 + G1_PAIR1)[r]
                    col = (BK if r % 4 >= 2 else 0) + r // 4
                    bias = vec[:, col:col + 1] if r % 4 >= 2 else bq8[:, r // 4:r // 4 + 1]
                    act.wait_ge(qk_stacked[r % 2], FREE_CREDIT + QK_IMAGE * i + qk_dma_before(r))
                    wait_acc(g1, a)
                    nc.scalar.activation(qk_hi[:, r % 2, :], acc_bank(a), ACT.Identity, bias=bias, scale=1.0)\
                        .then_inc(acc_high, 1)

                def v_high(v):
                    a = G1_V[v]
                    wait_acc(g1, a)
                    for j in range(2):
                        ins = nc.scalar.activation(v_st[:, 2 * v + j, :, 0, :],
                                                   acc[:, a % 2, j * C:(j + 1) * C].rearrange("p (h d) -> p h d", d=HD),
                                                   ACT.Copy)
                    ins.then_inc(acc_high, 1)

                def o_rows(j):
                    rows, a, slot = slice((j % 2) * HD, (j % 2 + 1) * HD), G1_AV[j], (j // 2) % 2
                    pair = (j // 2) % 2
                    wait_acc(g1, a)
                    if j % 2 == 0 and j >= 4:
                        act.wait_ge(o_split, FREE_CREDIT + 4 * i + j // 2 - 1)
                    if j % 2 == 0 and j < 4:
                        act.wait_ge(o_split, FREE_CREDIT + 4 * i)
                    nc.scalar.activation(o_sum[rows, slot, :], acc[HD:2 * HD, a % 2, :], ACT.Identity,
                                         bias=vec[rows, BV + pair:BV + pair + 1], scale=1.0).then_inc(o_part, 1)
                    if j % 2:
                        act.wait_ge(acc_evac, EVAC_CREDIT + g1 + a + 1)
                        nc.scalar.activation(o_hi[:, pair, :], o_sum[:, slot, :], ACT.Copy).then_inc(o_high, 1)

                for r in range(4):
                    qk_high(r)
                    v_high(r)
                for s in range(T1_IMAGE + LAG):
                    if s >= LAG:
                        t = s - LAG
                        j = t // 4
                        trans_high(t1, t, g1 + G1_AV[j - 2] if j >= 2 else g1 - G1_IMAGE + G1_AV[6 + j])
                    if s < T1_IMAGE:
                        exp(t1, s)
                    if 2 <= s <= 5:
                        qk_high(4 + s - 2)
                    if s - 2 in GN_STEPS:
                        norm_chunk_high(i + 1, GN_STEPS.index(s - 2))
                    if av1_after(s) is not None:
                        o_rows(av1_after(s))
                o_rows(7)

        @block.vector
        def _(dve):
            dve.sem_inc(acc_evac, EVAC_CREDIT)
            dve.sem_inc(xT_split, FREE_CREDIT)
            dve.sem_inc(pt_split, SPLIT_CREDIT)

            def row_max(t0, t):
                dve.wait_ge(scores_ready, t0 + t + 1)
                nc.vector.tensor_reduce(negmax[:, t % 2:t % 2 + 1], scores[:, t % 2, :], AX_X, ALU.max,
                                        negate=True).then_inc(max_ready, 1)

            def recip(t0, t):
                dve.wait_ge(exp_ready, EXP_CREDIT + t0 + t + 1)
                nc.vector.reciprocal(rsum[:, t % 2:t % 2 + 1], rowsum[:, t % 2:t % 2 + 1]).then_inc(rsum_ready, 1)

            def trans_low(t0, t):
                for h in range(2):
                    dve.wait_ge(pt_high, 2 * (t0 + t) + h + 1)
                    slot = (t // 4) % 2
                    nc.vector.tensor_tensor(pt_block(pt_lo, slot, t, h),
                                            trans[:, h, :].rearrange("p (j n) -> p j n", n=P),
                                            pt_block(pt_hi, slot, t, h).bitcast(F32),
                                            ALU.subtract).then_inc(pt_split, 1)

            def wait_acc(g0, a):
                dve.wait_ge(acc_done, GROUP_CREDIT + g0 + a + 1)

            for n, w in enumerate(WEIGHTS):
                dve.wait_ge(w_high, n + 1)
                if n == 2:
                    dve.wait_ge(x_high, 1)
                    nc.vector.tensor_tensor(flat(x_lo), flat(x_raw), flat(x_hi).bitcast(F32),
                                            ALU.subtract).then_inc(x_split, 1)
                nc.vector.scalar_tensor_tensor(flat(w_lo[w]), flat(w_raw[w]), QSCALE if w == "q" else 1.0,
                                               flat(w_hi[w]).bitcast(F32), ALU.mult, ALU.subtract).then_inc(w_split, 1)
            dve.wait_ge(vec_loaded, 16)
            nc.vector.tensor_scalar(bq8[:, :], vec[:, BQ:BQ + 2], QSCALE, None, ALU.mult).then_inc(w_split, 1)
            for ct in range(KT):
                dve.wait_ge(acc_high, ct + 1)
                nc.vector.tensor_tensor(wk_lo[:, ct, :], acc[:, ct, 0:C], wk_hi[:, ct, :].bitcast(F32),
                                        ALU.subtract).then_inc(acc_evac, 1)

            with dve.Fori(0, IMAGES) as i:
                g0, t0 = G0_BASE + G0_IMAGE * i, T0_IMAGE * i
                high0 = KT + 8 * i
                for a in range(4):
                    half, ct = a // 2, a % 2
                    cols = slice(half * H, (half + 1) * H)
                    dve.wait_ge(acc_high, high0 + a + 1)
                    nc.vector.tensor_tensor(a_lo[:, ct, cols], acc[:, a % 2, :], a_hi[:, ct, cols].bitcast(F32),
                                            ALU.subtract).then_inc(acc_evac, 1)
                for s in range(T0_IMAGE + LAG):
                    if 1 <= s <= T0_IMAGE:
                        recip(t0, s - 1)
                    if s < T0_IMAGE:
                        row_max(t0, s)
                    if s >= LAG:
                        trans_low(t0, s - LAG)
                    if s == 2:
                        dve.wait_ge(xT_high, i + 1)
                        nc.vector.tensor_tensor(flat(xT_lo), flat(xT_raw), flat(xT_hi).bitcast(F32),
                                                ALU.subtract).then_inc(xT_split, 1)
                    if s == T0_IMAGE:
                        dve.wait_ge(x_high, i + 2)
                        nc.vector.tensor_tensor(flat(x_lo), flat(x_raw), flat(x_hi).bitcast(F32),
                                                ALU.subtract).then_inc(x_split, 1)
                for n in range(4):
                    half, ct = n // 2, n % 2
                    cols = slice(half * H, (half + 1) * H)
                    dve.wait_ge(acc_high, high0 + 4 + n + 1)
                    nc.vector.tensor_tensor(u_lo[:, ct, cols], acc[:, n % 2, :], u_hi[:, ct, cols].bitcast(F32),
                                            ALU.subtract).then_inc(acc_evac, 1)
                dve.wait_ge(res_loaded, 64 * i + 64)
                for a in range(4):
                    half, o = a // 2, a % 2
                    wait_acc(g0, G0_OUT + a)
                    nc.vector.scalar_tensor_tensor(y_out[:, a, :], acc[:, a % 2, :], vec[:, GAMMA:GAMMA + 1],
                                                   y_out[:, a, :], ALU.mult, ALU.add).then_inc(acc_evac, 1)
                    dve.wait_ge(acc_evac, EVAC_CREDIT + g0 + G0_OUT + a + 1)
                    col = ((i * KT + o) * 2 + half) * 6
                    nc.vector.bn_stats(y_stats[:, bass.ds(col, 6)], y_out[:, a, :]).then_inc(y_ready, 1)

            dve.wait_ge(y_ready, 4 * IMAGES)
            mv = gn_mv[:, :, :, :].rearrange("p i k v -> p (i k) v")
            for n in range(IMAGES * KT):
                nc.vector.bn_aggr(mv[:, n, :], y_stats[:, n * 12:(n + 1) * 12]).then_inc(gn_stats, 1)
            links = [0]

            def link(ins):
                ins.then_inc(gn_chain, 1)
                links[0] += 1
                dve.wait_ge(gn_chain, links[0])

            mean = gn_mv[:, :, :, 0]
            gmean, gvar, inv, root, t1_, t2_ = (gn_tmp[:, n, :, :] for n in range(6))
            avg = acc[:, 0, 0:IMAGES * KT * 2].rearrange("p (i k v) -> p i k v", k=KT, v=2)
            wait_acc(0, GN_BASE)
            link(nc.vector.tensor_copy(gmean, avg[:, :, :, 0]))
            nc.vector.tensor_copy(gvar, avg[:, :, :, 1]).then_inc(acc_evac, 1)
            link(nc.vector.tensor_tensor(t1_, mean, gmean, ALU.subtract))
            nc.vector.tensor_tensor(t2_, t1_, t1_, ALU.mult).then_inc(gn_dev, 1)
            wait_acc(0, GN_BASE + 1)
            dev = acc[:, 1, 0:IMAGES * KT].rearrange("p (i k) -> p i k", k=KT)
            dve.wait_ge(acc_evac, EVAC_CREDIT + GN_BASE + 1)
            nc.vector.scalar_tensor_tensor(gvar, dev, EPS, gvar, ALU.add, ALU.add).then_inc(acc_evac, 1)
            dve.wait_ge(acc_evac, EVAC_CREDIT + GN_BASE + 2)
            nc.vector.reciprocal(inv, gvar).then_inc(gn_var, 1)
            dve.wait_ge(gn_sqrt, 1)
            link(nc.vector.tensor_tensor(t1_, root, root, ALU.mult))
            link(nc.vector.tensor_tensor(t1_, t1_, gvar, ALU.mult))
            link(nc.vector.tensor_scalar(t1_, t1_, -0.5, 1.5, ALU.mult, ALU.add))
            link(nc.vector.tensor_tensor(root, root, t1_, ALU.mult))
            for m in range(IMAGES + 1):
                n = m % IMAGES
                nc.vector.tensor_tensor(gn_scale[:, m, 0:KT], root[:, n, :], vec[:, GNW:GNW + KT], ALU.mult)\
                    .then_inc(gn_chain, 1)
                links[0] += 1
            dve.wait_ge(gn_chain, links[0])
            for m in range(IMAGES + 1):
                n = m % IMAGES
                ins = nc.vector.tensor_tensor(gn_scale[:, m, KT:2 * KT], gmean[:, n, :], gn_scale[:, m, 0:KT], ALU.mult)
                ins.then_inc(gn_chain, 1)
                links[0] += 1
            dve.wait_ge(gn_chain, links[0])
            for m in range(IMAGES + 1):
                ins = nc.vector.tensor_tensor(gn_scale[:, m, KT:2 * KT], vec[:, GNB:GNB + KT],
                                              gn_scale[:, m, KT:2 * KT], ALU.subtract)
                ins.then_inc(gn_chain, 1)
                links[0] += 1
            dve.wait_ge(gn_chain, links[0])
            nc.vector.tensor_copy(gn_now[:, :], gn_scale[:, 0, :]).then_inc(gn_affine, 1)

            with dve.Fori(0, IMAGES) as i:
                g1, t1 = G1_BASE + G1_IMAGE * i, T1_BASE + T1_IMAGE * i
                high1 = KT + 8 * IMAGES + 12 * i

                def qk_low(r):
                    a = (G1_PAIR0 + G1_PAIR1)[r]
                    bias = vec[:, BK + r // 4:BK + r // 4 + 1] if r % 4 >= 2 else bq8[:, r // 4:r // 4 + 1]
                    dve.wait_ge(acc_high, high1 + a + 1)
                    nc.vector.scalar_tensor_tensor(qk_lo[:, r % 2, :], acc[:, a % 2, :], bias,
                                                   qk_hi[:, r % 2, :].bitcast(F32),
                                                   ALU.add, ALU.subtract).then_inc(acc_evac, 1)

                def v_low(v):
                    a = G1_V[v]
                    dve.wait_ge(acc_high, high1 + a + 1)
                    for j in range(2):
                        ins = nc.vector.tensor_tensor(v_st[:, 2 * v + j, :, 1, :],
                                                      acc[:, a % 2, j * C:(j + 1) * C].rearrange("p (h d) -> p h d", d=HD),
                                                      v_st[:, 2 * v + j, :, 0, :].bitcast(F32), ALU.subtract)
                    ins.then_inc(acc_evac, 1)

                def o_add(j):
                    rows, a, slot = slice((j % 2) * HD, (j % 2 + 1) * HD), G1_AV[j], (j // 2) % 2
                    dve.wait_ge(o_part, 8 * i + j + 1)
                    nc.vector.tensor_tensor(o_sum[rows, slot, :], acc[0:HD, a % 2, :], o_sum[rows, slot, :],
                                            ALU.add).then_inc(acc_evac, 1)

                def result(n):
                    a, o = G1_OUT[n], n % 2
                    wait_acc(g1, a)
                    dve.wait_ge(yres_loaded, 64 * i + 32 * (n // 2) + 32)
                    nc.vector.scalar_tensor_tensor(y_res[:, o, :], acc[:, a % 2, :], vec[:, BP + o:BP + o + 1],
                                                   y_res[:, o, :], ALU.add, ALU.add).then_inc(acc_evac, 1)

                for r in range(4):
                    qk_low(r)
                    v_low(r)
                for s in range(T1_IMAGE + LAG):
                    if 1 <= s <= T1_IMAGE:
                        recip(t1, s - 1)
                    if s < T1_IMAGE:
                        row_max(t1, s)
                    if s >= LAG:
                        trans_low(t1, s - LAG)
                    if 2 <= s <= 5:
                        qk_low(4 + s - 2)
                    if s == 7:
                        dve.wait_ge(h_split, 4 * i + 4)
                        nc.vector.tensor_copy(gn_now[:, :], gn_scale[:, i + 1, :]).then_inc(gn_affine, 1)
                    if av1_after(s) is not None:
                        o_add(av1_after(s))
                    if s == OUT_STEP:
                        result(0)
                        result(1)
                o_add(7)
                result(2)
                result(3)

        @block.tensor
        def _(pe):
            pe.sem_inc(transposed, TRANS_CREDIT)
            pe.sem_inc(acc_done, GROUP_CREDIT)

            def group(g0, a, pairs, out_ap=None):
                pe.wait_ge(acc_evac, g0 + a + 1)
                dst = acc[:, a % 2, :] if out_ap is None else out_ap
                for n, (w, m) in enumerate(pairs):
                    ins = nc.tensor.matmul(dst, w, m, start=(n == 0), stop=(n == len(pairs) - 1))
                ins.then_inc(acc_done, 1)

            def evacuated(g0, a):
                pe.wait_ge(acc_evac, EVAC_CREDIT + g0 + a + 1)

            def over_k(w, m):
                return [pair for k in range(KT)
                        for pair in products((w(0, k), m(0, k)), (w(1, k), m(1, k)))]

            def transpose_tile(t0, t):
                pe.wait_ge(prob_ready, t0 + t + 1)
                for h in range(2):
                    pe.wait_ge(pt_split, 2 * (t0 + t) + h + 1)
                    for b in range(4):
                        j = 4 * h + b
                        ins = nc.tensor.transpose(trans[:, h, b * P:(b + 1) * P],
                                                  prob[:, t % 2, j * P:(j + 1) * P], ident[:, :])
                    ins.then_inc(transposed, 1)

            w = lambda name: (lambda part, k, cols: (w_hi, w_lo)[part][name][:, k, cols])
            wb, wc, wd, wq, wk, wv, wp = (w(n) for n in "bcdqkvp")
            abc = lambda part, k, cols: (wk_hi, wk_lo)[part][:, k, cols]
            col = lambda n, size: slice(n * size, (n + 1) * size)

            pe.wait_ge(w_split, 2)
            for ct in range(KT):
                group(0, ct, over_k(lambda part, k: wb(part, k, col(ct, P)),
                                    lambda part, k: wc(part, k, slice(0, C))), acc[:, ct, 0:C])
            pe.wait_ge(consts_ready, 5)
            pe.wait_ge(w_split, len(WEIGHTS))
            evacuated(0, 1)

            with pe.Fori(0, IMAGES) as i:
                g0, t0 = G0_BASE + G0_IMAGE * i, T0_IMAGE * i

                def values(n):
                    half, ct = n // 2, n % 2
                    if ct == 0:
                        pe.wait_ge(pt_split, SPLIT_CREDIT + 2 * t0 + 8 * (half + 1))
                    slot = half % 2
                    group(g0, G0_AV + n, [
                        pair for j in range(NT)
                        for pair in products((xT_hi[:, j, col(ct, P)], pt_hi[:, slot, j, :]),
                                             (xT_lo[:, j, col(ct, P)], pt_lo[:, slot, j, :]))])

                pe.wait_ge(x_split, i + 1)
                for a in range(4):
                    half, ct = a // 2, a % 2
                    group(g0, G0_A + a, over_k(
                        lambda part, k: abc(part, k, col(ct, P)),
                        lambda part, k: (x_hi, x_lo)[part][:, k, col(half, H)]))
                for s in range(T0_IMAGE + LAG):
                    if s < T0_IMAGE:
                        if s % 4 == 0:
                            evacuated(g0, G0_A + 2 * (s // 4) + 1)
                        pe.wait_ge(exp_ready, t0 + s + 1)
                        for mh in range(2):
                            pairs = over_k(lambda part, k: (a_hi, a_lo)[part][:, k, col(s, P)],
                                           lambda part, k: (x_hi, x_lo)[part][:, k, col(mh, H)])
                            for n, (l, r) in enumerate(pairs):
                                ins = nc.tensor.matmul(scores[:, s % 2, col(mh, H)], l, r, start=(n == 0),
                                                       stop=(n == len(pairs) - 1))
                        ins.then_inc(scores_ready, 1)
                    if s >= LAG:
                        transpose_tile(t0, s - LAG)
                    if s == T0_IMAGE - 1:
                        pe.wait_ge(xT_split, FREE_CREDIT + i + 1)
                        values(0)
                for n in range(1, 4):
                    values(n)
                for a in range(4):
                    half, o = a // 2, a % 2
                    evacuated(g0, G0_AV + 2 * half + 1)
                    group(g0, G0_OUT + a, over_k(
                        lambda part, k: wd(part, k, col(o, P)),
                        lambda part, k: (u_hi, u_lo)[part][:, k, col(half, H)]))

            pe.wait_ge(gn_stats, IMAGES * KT)
            n_mv = IMAGES * KT * 2
            group(0, GN_BASE, [(gavg[:, :], gn_mv[:, :, :, :].rearrange("p i k v -> p (i k v)"))],
                  acc[:, 0, 0:n_mv])
            pe.wait_ge(gn_dev, 1)
            group(0, GN_BASE + 1, [(gavg[:, :], gn_tmp[:, 5, :, :].rearrange("p i k -> p (i k)"))],
                  acc[:, 1, 0:n_mv // 2])

            with pe.Fori(0, IMAGES) as i:
                g1, t1 = G1_BASE + G1_IMAGE * i, T1_BASE + T1_IMAGE * i
                h_part = lambda part, k, cols: (h_hi, h_lo)[part][:, k, cols]

                def project_qk(r):
                    pair, half = r // 4, r % 2
                    wt = wk if r % 4 >= 2 else wq
                    group(g1, (G1_PAIR0 + G1_PAIR1)[r], over_k(
                        lambda part, k: wt(part, k, col(pair, P)),
                        lambda part, k: h_part(part, k, col(half, H))))

                def project_v(v):
                    a = G1_V[v]
                    pe.wait_ge(acc_evac, g1 + a + 1)
                    for j in range(2):
                        pairs = over_k(lambda part, k: h_part(part, k, col(2 * v + j, P)),
                                       lambda part, k: wv(part, k, slice(0, C)))
                        for n, (l, r) in enumerate(pairs):
                            ins = nc.tensor.matmul(acc[:, a % 2, col(j, C)], l, r, start=(n == 0),
                                                   stop=(n == len(pairs) - 1))
                    ins.then_inc(acc_done, 1)

                def values(j, part):
                    a, head, slot = G1_AV[j], j % 4, j % 2
                    if part == 0:
                        pe.wait_ge(pt_split, SPLIT_CREDIT + 2 * t1 + 8 * (j + 1))
                        pe.wait_ge(acc_evac, g1 + a + 1)
                    for b in range(2 * part, 2 * part + 2):
                        v = v_st[:, b, head, :, :].rearrange("p v d -> p (v d)")
                        for n, src in enumerate((pt_hi, pt_lo)):
                            last = b == NT - 1 and n == 1
                            ins = nc.tensor.matmul(acc[:, a % 2, :], v, src[:, slot, b, :],
                                                   start=(b == 0 and n == 0), stop=last)
                    if last:
                        ins.then_inc(acc_done, 1)

                def project_out(n):
                    half, o = n // 2, n % 2
                    group(g1, G1_OUT[n], over_k(
                        lambda part, k: wp(part, k, col(o, P)),
                        lambda part, k: (o_hi, o_lo)[part][:, k, :]))

                pe.wait_ge(h_split, 4 * i + 4)
                for r in range(4):
                    project_qk(r)
                    project_v(r)
                for s in range(T1_IMAGE + LAG):
                    if s < T1_IMAGE:
                        half, head, tile = s // 16, (s // 4) % 4, 4 * (s // 16) + s % 4
                        if s in (0, 8):
                            for slot in range(2):
                                pe.wait_ge(qk_stacked[slot], FREE_CREDIT + QK_IMAGE * i + qk_dma_before(4 if s == 0 else 8))
                        pe.wait_ge(exp_ready, t1 + s + 1)
                        for mh in range(2):
                            for part in range(2):
                                ins = nc.tensor.matmul(scores[:, s % 2, col(mh, H)], q_st[:, head, col(tile, P)],
                                                       k_st[:, part, head, col(mh, H)],
                                                       start=(part == 0), stop=(part == 1))
                        ins.then_inc(scores_ready, 1)
                    if s >= LAG:
                        transpose_tile(t1, s - LAG)
                    if 2 <= s <= 5:
                        project_qk(4 + s - 2)
                    if s >= 6:
                        values((s - 6) // 4, (s - 6) % 4)
                    if s == OUT_STEP:
                        pe.wait_ge(o_split, FREE_CREDIT + 4 * i + 2)
                        project_out(0)
                        project_out(1)
                for part in range(4):
                    values(7, part)
                pe.wait_ge(o_split, FREE_CREDIT + 4 * i + 4)
                project_out(2)
                project_out(3)


_IN = {"x": "x", "b": "L0_conv_Wb", "c": "L0_conv_Wc", "d": "L0_conv_Wd", "q": "L1_conv_wq",
       "k": "L1_conv_wk", "v": "L1_conv_wv", "p": "L1_conv_wp"}


def kernel(**inputs):
    import numpy as np
    import concourse.bacc as bacc
    from concourse.bass_utils import run_bass_kernel_spmd

    x = np.ascontiguousarray(inputs["x"])
    arrays = {
        "in_x": x.reshape(IMAGES, KT, P, N),
        "in_xT": np.ascontiguousarray(x.reshape(IMAGES, C, N).transpose(0, 2, 1)),
    }
    for w in WEIGHTS:
        a = np.asarray(inputs[_IN[w]])
        arrays[f"in_w{w}"] = np.ascontiguousarray(a if w in "bc" else a.T)
    columns = [np.asarray(inputs[n]).reshape(KT, P).T for n in (
        "L1_conv_bq", "L1_conv_bk", "L1_conv_bv", "L1_conv_bp", "L1_conv_gamma", "L1_conv_beta")]
    columns.append(np.broadcast_to(np.asarray(inputs["L0_conv_gamma"]).reshape(1, 1), (P, 1)))
    arrays["in_vecs"] = np.ascontiguousarray(np.concatenate(columns, axis=1))

    nc = bacc.Bacc("TRN2", target_bir_lowering=False, num_devices=1)
    t = {n: nc.dram_tensor(n, a.shape, F32, kind="ExternalInput").ap() for n, a in arrays.items()}
    out = nc.dram_tensor("out_0", (IMAGES, KT, P, N), F32, kind="ExternalOutput").ap()
    build(nc, t["in_x"], t["in_xT"], {w: t[f"in_w{w}"] for w in WEIGHTS}, t["in_vecs"], out)
    r = run_bass_kernel_spmd(nc, [arrays], core_ids=[0])
    return r.results[0]["out_0"].reshape(IMAGES, C, 32, 32)
```

```python
from contextlib import ExitStack

import concourse.bass as bass
from concourse import mybir

F32 = mybir.dt.float32
F32R = mybir.dt.float32r
ALU = mybir.AluOpType
ACT = mybir.ActivationFunctionType
AX_X = mybir.AxisListType.X

P = 128
IMAGES = 4
C = 256
KT = C // P
N = 1024
H = 512
NT = N // P
HEADS = 4
HD = C // HEADS
PAIRS = HEADS // 2
GROUP = C // 32
EPS = 1e-5
QSCALE = HD ** -0.5

T0_IMAGE = NT
T1_IMAGE = HEADS * NT
T1_BASE = IMAGES * T0_IMAGE
LAG = 2

FIRST_A = ["a0", "a1", "a2", "a3"]
TAIL0 = ["av0", "t6", "av1", "t7", "y0", "y1", "av2", "next_a0", "av3", "next_a1",
         "y2", "next_a2", "y3", "next_a3"]
TAIL0_LAST = ["av0", "t6", "next_qk0", "av1", "t7", "next_qk1", "y0", "y1", "av2", "next_qk2",
              "av3", "next_qk3", "y2", "next_qk4", "y3", "next_qk5"]
LAYER0 = [n for n in TAIL0 if n not in ("t6", "t7")]
LAYER0_LAST = ["gn0", "gn1"] + [n for n in TAIL0_LAST if n not in ("t6", "t7")]

STEPS1 = {
    0: ["first_qk6"], 1: ["qk7"], 2: ["v0"], 3: ["v1"], 5: ["v2"], 6: ["v3"],
    7: ["prev_out2"], 9: [("prev_out3", 0, 3)], 10: [("prev_out3", 1, 3)],
    11: [("prev_out3", 2, 3)], 13: ["first_gn0"], 15: ["first_gn1"],
    21: ["next_qk0"], 22: ["out0"], 23: ["next_qk1"], 25: ["next_qk2"], 26: ["next_qk3"],
    27: ["out1"], 29: ["next_qk4"], 30: ["next_qk5"], 31: ["next_qk6"],
}
AV_PARTS = 4
for step in range(T1_IMAGE):
    head_half = (step // AV_PARTS - 1) % 8
    av = ("prev_" if step < AV_PARTS else "") + f"av{head_half}"
    STEPS1.setdefault(step, []).append((av, step % AV_PARTS, AV_PARTS))
STEPS1_ALL = [g for step in range(T1_IMAGE) for g in STEPS1[step]]
LAYER1 = [g if isinstance(g, str) else g[0] for g in STEPS1_ALL if isinstance(g, str) or g[1] == g[2] - 1]
PAIR_ENDS = ["prev_av7", "av1", "av3", "av5"]
SUM_BEHIND, PAIR_BEHIND = 1, 2
EPILOGUE = ["prev_av7", "prev_out2", "prev_out3"]
STEP_EPILOGUE = [("prev_out2", 0, 2), "prev_av7", ("prev_out2", 1, 2), "prev_out3"]
NORM_STEPS0 = [3, 4, 5, 6]
NORM_STEPS1 = [7, 10, 14, 17]
X_HALVES = 2
XT_PARTS = 4
XT_STEPS = [2, 3, 4, 5]


class Plan:

    def __init__(self, names, base, parity, first=False, last=False, ring=True):
        self.names = [n for n in names if not (first and n.startswith("prev_"))
                      and not (last and n.startswith("next_"))
                      and (first or not n.startswith("first_"))]
        self.base, self.parity, self.first, self.last, self.ring = base, parity, first, last, ring

    def has(self, name):
        return name in self.names

    def number(self, name):
        return self.base + self.names.index(name)

    def bank(self, name):
        if not self.ring:
            is_av = [n for n in self.names[self.names.index(name):] if "av" in n]
            if name in is_av or not is_av:
                return int(name[-1]) % 2
            return 1 - int(is_av[0][-1]) % 2
        return (self.parity + self.names.index(name)) % 2

    def before(self, name):
        if self.ring:
            return self.number(name) - 2
        same = [n for n in self.names[:self.names.index(name)] if self.bank(n) == self.bank(name)]
        if same:
            return self.number(same[-1])
        return self.base - (2 if name == "prev_av7" else 1)

    def until(self, name, kinds):
        return sum(n.removeprefix("prev_").removeprefix("next_").removeprefix("first_").startswith(kinds)
                   for n in self.names[:self.names.index(name) + 1])


PLAN_FIRST_A = Plan(FIRST_A, KT, KT)
BASE0 = KT + len(FIRST_A)
BASE1 = BASE0 + (IMAGES - 1) * len(LAYER0) + len(LAYER0_LAST)
PLAN1_FIRST = Plan(LAYER1, BASE1, BASE1, first=True, ring=False)
BASE1_MID = BASE1 + len(PLAN1_FIRST.names)
GROUPS1 = len(Plan(LAYER1, 0, 0).names)
BASE1_LAST = BASE1_MID + (IMAGES - 2) * GROUPS1
PLAN1_LAST = Plan(LAYER1, BASE1_LAST, BASE1_LAST, last=True, ring=False)
BASE_EPILOGUE = BASE1_LAST + len(PLAN1_LAST.names)
PLAN_EPILOGUE = Plan(EPILOGUE, BASE_EPILOGUE, BASE_EPILOGUE, ring=False)


def plan0(i, last=False):
    return Plan(LAYER0_LAST if last else LAYER0, BASE0 + len(LAYER0) * i, BASE0)


def plan1(i):
    if isinstance(i, int) and i == 0:
        return PLAN1_FIRST
    if isinstance(i, int) and i == IMAGES - 1:
        return PLAN1_LAST
    return Plan(LAYER1, BASE1_MID + GROUPS1 * (i - 1), BASE1_MID, ring=False)


EXP_CREDIT = 2
TRANS_CREDIT = 4
SPLIT_CREDIT = 2
GROUP_CREDIT = 6
EVAC_CREDIT = 2

FREE_CREDIT = 1

BQ, BK, BV, BP, GNW, GNB, GAMMA = 0, 2, 4, 6, 8, 10, 12
NVEC = 13
GN_SETS = [(0, IMAGES - 1), (IMAGES - 1, IMAGES)]
WEIGHTS = ["b", "c", "d", "q", "k", "v", "p"]
LATER_WEIGHTS = WEIGHTS[2:]


def products(his, los):
    (ah, bh), (al, bl) = his, los
    return [(ah, bh), (al, bh), (ah, bl)]


def build(nc, x, xT, weights, vecs, out):
    y_dram = nc.dram_tensor("y_scratch", (IMAGES, KT, P, N), F32, kind="Internal").ap()
    ctx = ExitStack()
    with ctx:
        def sb(name, shape, dt=F32, scope=ctx):
            return scope.enter_context(nc.sbuf_tensor(name, shape, dt))

        def sem(name):
            return ctx.enter_context(nc.semaphore(name))

        vec = sb("vec", [P, NVEC])
        bq8 = sb("bq8", [P, 2])
        ident = sb("ident", [P, P])
        gavg = sb("gavg", [P, P])
        gn_mv = sb("gn_mv", [P, IMAGES, KT, 2])
        gn_mean = sb("gn_mean", [P, IMAGES, KT])
        gn_var = sb("gn_var", [P, IMAGES, KT])
        gn_root = sb("gn_root", [P, IMAGES, KT])
        gn_dev = sb("gn_dev", [P, IMAGES, KT])
        gn_sqdev = sb("gn_sqdev", [P, IMAGES, KT])
        minus_half = sb("minus_half", [P, IMAGES, KT])
        gn_scale = sb("gn_scale", [P, IMAGES, 2 * KT])
        gn_now = sb("gn_now", [P, 2 * KT])
        y_stats = sb("y_stats", [P, IMAGES * KT * 2 * 6])
        negmax = sb("negmax", [P, 2])
        rowsum = sb("rowsum", [P, 2])
        rsum = sb("rsum", [P, 2])
        w_hi = {w: sb(f"w{w}_hi", [P, KT, C], F32R) for w in "dqkvp"}
        w_lo = {w: sb(f"w{w}_lo", [P, KT, C], F32R) for w in "dqkvp"}
        start = ExitStack()
        w_raw = {w: sb(f"w{w}_raw", [P, KT, C], F32, start) for w in "bc"}
        w_later = sb("w_later", [P, len(LATER_WEIGHTS), KT, C], F32, start)
        w_raw.update({w: w_later[:, n, :, :] for n, w in enumerate(LATER_WEIGHTS)})
        bc_hi = {w: sb(f"w{w}_hi", [P, KT, C], F32R, start) for w in "bc"}
        bc_lo = {w: sb(f"w{w}_lo", [P, KT, C], F32R, start) for w in "bc"}
        start.close()
        w_hi.update(bc_hi)
        w_lo.update(bc_lo)
        pt_hi = sb("pt_hi", [P, 2, NT, H], F32R)
        pt_lo = sb("pt_lo", [P, 2, NT, H], F32R)
        prob = sb("prob", [P, 2, N])
        h_hi = sb("h_hi", [P, KT, N], F32R)
        h_lo = sb("h_lo", [P, KT, N], F32R)
        y_in = sb("y_in", [P, KT, 2, H])

        layer0 = ExitStack()
        a_hi = sb("a_hi", [P, KT, N], F32R, layer0)
        a_lo = sb("a_lo", [P, KT, N], F32R, layer0)
        x_raw = sb("x_raw", [P, KT, N], F32, layer0)
        x_hi = sb("x_hi", [P, KT, N], F32R, layer0)
        x_lo = sb("x_lo", [P, KT, N], F32R, layer0)
        wk_hi = sb("wbc_hi", [P, KT, C], F32R, layer0)
        wk_lo = sb("wbc_lo", [P, KT, C], F32R, layer0)
        xT_raw = sb("xT_raw", [P, NT, C], F32, layer0)
        sb("unused", [P, C * KT * 2], F32, layer0)
        xT_hi = sb("xT_hi", [P, NT, C], F32R, layer0)
        xT_lo = sb("xT_lo", [P, NT, C], F32R, layer0)
        u_hi = sb("u_hi", [P, KT, H], F32R, layer0)
        u_lo = sb("u_lo", [P, KT, H], F32R, layer0)
        y_out = sb("y_out", [P, 4, H], F32, layer0)
        layer0.close()

        q_st = sb("q_st", [P, HEADS, N], F32R)
        k_st = sb("k_st", [P, 2, HEADS, N], F32R)
        qk = sb("qk", [P, 2, 2, H], F32R)
        v_st = sb("v_st", [P, NT, HEADS, 2, HD], F32R)
        o_sum = sb("o_sum", [P, 2, H])
        o_hi = sb("o_hi", [P, KT, H], F32R)
        o_lo = sb("o_lo", [P, KT, H], F32R)
        y_res = sb("y_res", [P, 2, H])

        scores = ctx.enter_context(nc.psum_tensor("scores", [P, 2, N], F32))
        trans = ctx.enter_context(nc.psum_tensor("trans", [P, 2, H], F32))
        acc = ctx.enter_context(nc.psum_tensor("acc", [P, 2, H], F32))

        consts_ready = sem("consts_ready")
        vec_loaded = sem("vec_loaded")
        w_loaded = sem("w_loaded")
        later_loaded = sem("later_loaded")
        w_high = sem("w_high")
        w_split = sem("w_split")
        x_loaded = [sem("x_loaded0"), sem("x_loaded1")]
        x_high = sem("x_high")
        x_split = sem("x_split")
        xT_loaded = sem("xT_loaded")
        xT_high = sem("xT_high")
        xT_split = sem("xT_split")
        res_loaded = sem("res_loaded")
        y_summed = sem("y_summed")
        y_ready = sem("y_ready")
        y_stored = sem("y_stored")
        scores_ready = sem("scores_ready")
        max_ready = sem("max_ready")
        exp_ready = sem("exp_ready")
        rsum_ready = sem("rsum_ready")
        prob_ready = sem("prob_ready")
        transposed = sem("transposed")
        pt_high = sem("pt_high")
        pt_split = sem("pt_split")
        acc_done = sem("acc_done")
        acc_high = sem("acc_high")
        acc_evac = sem("acc_evac")
        gn_chain = sem("gn_chain")
        gn_var_ready = sem("gn_var_ready")
        gn_root_ready = sem("gn_root_ready")
        gn_stats = sem("gn_stats")
        gn_dev_ready = sem("gn_dev_ready")
        gn_affine = sem("gn_affine")
        y_loaded = sem("y_loaded")
        h_full = sem("h_full")
        h_high = sem("h_high")
        h_split = sem("h_split")
        qk_stacked = [sem("qk_stacked0"), sem("qk_stacked1")]
        o_part = sem("o_part")
        o_high = sem("o_high")
        o_split = sem("o_split")
        yres_loaded = sem("yres_loaded")
        out_stored = sem("out_stored")
        pool_steps = sem("pool_steps")

        CHUNK_DMA = 4 * 16
        QK_IMAGE = 4 * CHUNK_DMA

        def image_groups(step):
            return [g if isinstance(g, str) else g[0] for g in step
                    if isinstance(g, str) or g[1] == g[2] - 1]

        def head_outputs(step):
            return [name for name in image_groups(step) if "av" in name]

        def other_groups(step):
            return [name for name in image_groups(step) if "av" not in name]

        def pair_difference(engine, pair):
            engine.tensor_tensor(o_lo[:, pair, :], o_sum[:, pair, :], o_hi[:, pair, :].bitcast(F32),
                                 ALU.subtract).then_inc(o_split, 1)

        def flat(ap):
            return ap.rearrange("p a b -> p (a b)")

        def pt_block(buf, half_slot, t, h):
            return buf[:, half_slot, 4 * h:4 * h + 4, (t % 4) * P:(t % 4 + 1) * P]

        def xT_part(buf, s):
            n, size = XT_STEPS.index(s), NT // XT_PARTS
            return buf[:, n * size:(n + 1) * size, :].rearrange("p a b -> p (a b)")

        def qk_bias(r):
            return vec[:, BK + r // 4:BK + r // 4 + 1] if r % 4 >= 2 else bq8[:, r // 4:r // 4 + 1]

        block = ctx.enter_context(nc.Block())

        @block.sync
        def _(sp):
            for s in (y_stored, out_stored, *qk_stacked):
                sp.sem_inc(s, FREE_CREDIT)
            for w in "bc":
                sp.dma_start(w_raw[w][:, :, :], weights[w].rearrange("(k p) c -> p k c", p=P)).then_inc(w_loaded, 16)

            def load_x(i):
                for half in range(X_HALVES):
                    cols = slice(half * H, (half + 1) * H)
                    sp.dma_start(x_raw[:, :, cols], x[i, :, :, cols].rearrange("k p n -> p k n")).then_inc(x_loaded[half], 16)

            load_x(0)
            sp.dma_start(vec[:, :], vecs).then_inc(vec_loaded, 16)
            sp.dma_start(w_later[:, :, :, :].rearrange("p w k c -> p (w k) c"),
                         weights["later"].rearrange("w p c -> p w c")).then_inc(later_loaded, 16)

            def evacuated(plan, name):
                sp.wait_ge(acc_evac, EVAC_CREDIT + plan.number(name) + 1)

            def restack(plan, name):
                r = int(name[-1])
                pair, is_k, half, slot = r // 4, r % 4 >= 2, r % 2, r % 2
                cols = slice(half * H, (half + 1) * H)
                evacuated(plan, name)
                for n in range(2):
                    head, rows = 2 * pair + n, slice(n * HD, (n + 1) * HD)
                    for u in range(2):
                        if is_k:
                            dst, src = k_st[u * HD:(u + 1) * HD, :, head, cols], qk[rows, slot, :, :]
                        else:
                            dst, src = q_st[u * HD:(u + 1) * HD, head, cols], qk[rows, slot, u, :]
                        sp.dma_start(dst.bitcast(F32), src.bitcast(F32)).then_inc(qk_stacked[slot], 16)

            def load_y(i):
                sp.dma_start(y_in[:, :, :, :], y_dram[i].rearrange("k p (a n) -> p k a n", a=2)).then_inc(y_loaded, 16)

            def image0(i, last):
                plan = plan0(i, last)
                sp.wait_ge(xT_split, FREE_CREDIT + XT_PARTS * i)
                sp.dma_start(xT_raw[:, :, :], xT[i].rearrange("(j p) c -> p j c", p=P)).then_inc(xT_loaded, 16)
                sp.wait_ge(y_stored, FREE_CREDIT + i * 64)
                for a in range(4):
                    sp.dma_start(y_out[:, a, :], x[i, a % 2, :, (a // 2) * H:(a // 2 + 1) * H]).then_inc(res_loaded, 16)
                if last:
                    load_y(0)
                else:
                    sp.wait_ge(x_split, X_HALVES * (i + 1))
                    load_x(i + 1)
                for name in plan.names:
                    if name.startswith("next_qk"):
                        restack(plan, name)
                    elif name.startswith("y"):
                        a = int(name[-1])
                        sp.wait_ge(y_ready, 4 * i + a + 1)
                        sp.dma_start(y_dram[i, a % 2, :, (a // 2) * H:(a // 2 + 1) * H], y_out[:, a, :])\
                            .then_inc(y_stored, 16)

            with sp.Fori(0, IMAGES - 1) as i:
                image0(i, False)
            image0(IMAGES - 1, True)

            def load_residual(i, half):
                sp.wait_ge(out_stored, FREE_CREDIT + 64 * i + 32 * half)
                for o in range(2):
                    sp.dma_start(y_res[:, o, :], y_dram[i, o, :, half * H:(half + 1) * H]).then_inc(yres_loaded, 16)

            def store(plan, name, i):
                n = int(name[-1])
                evacuated(plan, name)
                sp.dma_start(out[i, n % 2, :, (n // 2) * H:(n // 2 + 1) * H], y_res[:, n % 2, :]).then_inc(out_stored, 16)

            def image1(i):
                plan = plan1(i)
                if plan.first:
                    restack(plan, "first_qk6")
                    sp.wait_ge(y_stored, FREE_CREDIT + IMAGES * 64)
                restack(plan, "qk7")
                if not plan.last:
                    sp.wait_ge(h_split, 4 * i + 4)
                    load_y(i + 1)
                if not plan.first:
                    store(plan, "prev_out2", i - 1)
                    store(plan, "prev_out3", i - 1)
                load_residual(i, 0)
                for name in plan.names:
                    if name.startswith("next_qk"):
                        restack(plan, name)
                    elif name.startswith("out"):
                        store(plan, name, i)
                load_residual(i, 1)

            image1(0)
            with sp.Fori(1, IMAGES - 1) as i:
                image1(i)
            image1(IMAGES - 1)
            store(PLAN_EPILOGUE, "prev_out2", IMAGES - 1)
            store(PLAN_EPILOGUE, "prev_out3", IMAGES - 1)
            sp.wait_ge(out_stored, FREE_CREDIT + IMAGES * 64)

        @block.gpsimd
        def _(pool):
            pool.sem_inc(o_split, FREE_CREDIT)
            nc.gpsimd.memset(ident[:, :], 0.0).then_inc(consts_ready, 1)
            nc.gpsimd.memset(gavg[:, :], 1.0 / GROUP).then_inc(consts_ready, 1)
            pool.wait_ge(consts_ready, 2)
            nc.gpsimd.affine_select(out=ident[:, :], in_=ident[:, :], compare_op=ALU.not_equal, fill=1.0,
                                    base=0, pattern=[[-1, P]], channel_multiplier=1).then_inc(consts_ready, 1)
            groups = gavg[:, :].rearrange("p (g c) -> p g c", c=GROUP)
            nc.gpsimd.affine_select(out=groups, in_=groups, compare_op=ALU.is_ge, fill=0.0, base=0,
                                    pattern=[[-GROUP, P // GROUP], [0, GROUP]], channel_multiplier=1).then_inc(consts_ready, 1)
            nc.gpsimd.memset(minus_half[:, :, :], -0.5).then_inc(consts_ready, 1)
            pool.wait_ge(consts_ready, 5)
            nc.gpsimd.affine_select(out=groups, in_=groups, compare_op=ALU.is_ge, fill=0.0, base=GROUP - 1,
                                    pattern=[[GROUP, P // GROUP], [0, GROUP]], channel_multiplier=-1).then_inc(consts_ready, 1)

            def wait_scalar(semaphore, value):
                pool.wait_ge(semaphore, value)
                pool.sem_inc(pool_steps, 1)

            def normalise(t0, t):
                wait_scalar(rsum_ready, t0 + t + 1)
                p = prob[:, t % 2, :]
                nc.gpsimd.tensor_scalar(p, p, rsum[:, t % 2:t % 2 + 1], 1.0, ALU.mult, ALU.mult)\
                    .then_inc(prob_ready, 1)

            def norm_chunk(n, c):
                k, half = c // 2, c % 2
                if c == 0:
                    wait_scalar(y_loaded, 16 * n + 16)
                    wait_scalar(gn_affine, n + 1)
                y = y_in[:, k, half, :]
                nc.gpsimd.tensor_scalar(y, y, gn_now[:, k:k + 1], gn_now[:, KT + k:KT + k + 1],
                                        ALU.mult, ALU.add).then_inc(h_full, 1)

            def norm_chunk_low(n, c):
                k, half = c // 2, c % 2
                pool.wait_ge(h_high, 4 * n + c + 1)
                dst = slice(half * H, (half + 1) * H)
                nc.gpsimd.tensor_tensor(h_lo[:, k, dst], y_in[:, k, half, :], h_hi[:, k, dst].bitcast(F32),
                                        ALU.subtract).then_inc(h_split, 1)

            def norm_root(n):
                images = slice(*GN_SETS[n])
                pool.wait_ge(gn_var_ready, n + 1)
                nc.gpsimd.tensor_tensor(gn_root[:, images, :], gn_var[:, images, :], minus_half[:, images, :],
                                        ALU.pow).then_inc(gn_root_ready, 1)

            def norm_step(n, steps, s, behind):
                if s - behind in steps:
                    norm_chunk_low(n, steps.index(s - behind))
                if s in steps:
                    norm_chunk(n, steps.index(s))

            with pool.Fori(0, IMAGES - 1) as i:
                for t in range(T0_IMAGE):
                    normalise(T0_IMAGE * i, t)
            for t in range(T0_IMAGE):
                if t == 2:
                    norm_root(0)
                normalise(T0_IMAGE * (IMAGES - 1), t)
                norm_step(0, NORM_STEPS0, t, 1)
            normalise(T1_BASE, 0)

            def pair_low(i, j):
                pool.wait_ge(o_high, 4 * i + j // 2 + 1)
                pair_difference(nc.gpsimd, (j // 2) % 2)

            def pairs_of(i, names):
                for name in names:
                    if name in PAIR_ENDS:
                        pair_low(i - 1 if name == "prev_av7" else i, int(name[-1]))

            def image1(i):
                plan = plan1(i)
                for s in range(T1_IMAGE):
                    if s + 1 < T1_IMAGE or not plan.last:
                        normalise(T1_BASE + T1_IMAGE * i, s + 1)
                    if plan.first and s == 17:
                        norm_root(1)
                    if not plan.last:
                        norm_step(i + 1, NORM_STEPS1, s, 2)
                    if s >= PAIR_BEHIND:
                        pairs_of(i, [name for name in head_outputs(STEPS1[s - PAIR_BEHIND]) if plan.has(name)])

            image1(0)
            with pool.Fori(1, IMAGES - 1) as i:
                image1(i)
            image1(IMAGES - 1)

        @block.scalar
        def _(act):
            act.sem_inc(exp_ready, EXP_CREDIT)

            def wait_acc(number):
                act.wait_ge(acc_done, GROUP_CREDIT + number + 1)

            def exp(t0, t):
                act.wait_ge(max_ready, t0 + t + 1)
                act.wait_ge(transposed, TRANS_CREDIT + 2 * (t0 + t) - 2)
                nc.scalar.activation(prob[:, t % 2, :], scores[:, t % 2, :], ACT.Exp,
                                     bias=negmax[:, t % 2:t % 2 + 1], scale=1.0,
                                     accum_out=rowsum[:, t % 2:t % 2 + 1]).then_inc(exp_ready, 1)

            def trans_high(t0, t, av_before):
                if t % 4 == 0 and av_before is not None:
                    wait_acc(av_before)
                for h in range(2):
                    act.wait_ge(transposed, TRANS_CREDIT + 2 * (t0 + t) + h + 1)
                    nc.scalar.activation(pt_block(pt_hi, (t // 4) % 2, t, h),
                                         trans[:, h, :].rearrange("p (j n) -> p j n", n=P),
                                         ACT.Copy).then_inc(pt_high, 1)

            def weight_high(w):
                nc.scalar.activation(flat(w_hi[w]), flat(w_raw[w]), ACT.Copy,
                                     scale=QSCALE if w == "q" else 1.0).then_inc(w_high, 1)

            def x_part_high(i, half):
                act.wait_ge(x_loaded[half], 16 * i + 16)
                cols = slice(half * H, (half + 1) * H)
                nc.scalar.activation(x_hi[:, :, cols], x_raw[:, :, cols], ACT.Copy).then_inc(x_high, 1)

            def high(dst, plan, name):
                wait_acc(plan.number(name))
                nc.scalar.activation(dst, acc[:, plan.bank(name), :], ACT.Copy).then_inc(acc_high, 1)

            def a_high(plan, name):
                a = int(name[-1])
                high(a_hi[:, a % 2, (a // 2) * H:(a // 2 + 1) * H], plan, name)

            act.wait_ge(w_loaded, 2 * 16)
            weight_high("b")
            weight_high("c")
            x_part_high(0, 0)
            for ct in range(KT):
                wait_acc(ct)
                nc.scalar.activation(wk_hi[:, ct, :], acc[:, ct, 0:C], ACT.Copy).then_inc(acc_high, 1)
            x_part_high(0, 1)
            act.wait_ge(later_loaded, 16)
            for name, w in zip(FIRST_A, LATER_WEIGHTS):
                a_high(PLAN_FIRST_A, name)
                weight_high(w)
            weight_high(LATER_WEIGHTS[-1])

            def chunk_high(plan, name, i):
                r = int(name[-1])
                act.wait_ge(qk_stacked[r % 2], FREE_CREDIT + QK_IMAGE * i + CHUNK_DMA * (r // 2))
                wait_acc(plan.number(name))
                nc.scalar.activation(qk[:, r % 2, 0, :], acc[:, plan.bank(name), :], ACT.Identity,
                                     bias=qk_bias(r), scale=1.0).then_inc(acc_high, 1)

            def norm_chunk_high(n, c):
                k, half = c // 2, c % 2
                act.wait_ge(h_full, 4 * n + c + 1)
                nc.scalar.activation(h_hi[:, k, half * H:(half + 1) * H], y_in[:, k, half, :], ACT.Copy)\
                    .then_inc(h_high, 1)

            def image0(i, last):
                plan, t0 = plan0(i, last), T0_IMAGE * i

                def trans(t):
                    before = BASE0 + len(LAYER0) * (i - 1) + LAYER0.index("av3" if t >= 4 else "av1")
                    trans_high(t0, t, before)

                for s in range(T0_IMAGE):
                    if s >= LAG:
                        trans(s - LAG)
                    exp(t0, s)
                    if last and s - 1 in NORM_STEPS0:
                        norm_chunk_high(0, NORM_STEPS0.index(s - 1))
                    if s in XT_STEPS:
                        if s == XT_STEPS[0]:
                            act.wait_ge(xT_loaded, 16 * i + 16)
                        nc.scalar.activation(xT_part(xT_hi, s), xT_part(xT_raw, s), ACT.Copy).then_inc(xT_high, 1)
                for name in TAIL0_LAST if last else TAIL0:
                    n = int(name[-1])
                    if name.startswith("t"):
                        trans(n)
                        if name == "t7" and not last:
                            for half in range(X_HALVES):
                                x_part_high(i + 1, half)
                    elif name.startswith("av"):
                        high(u_hi[:, n % 2, :], plan, name)
                    elif name.startswith("next_a"):
                        a_high(plan, name)
                    elif name.startswith("next_qk"):
                        chunk_high(plan, name, 0)

            with act.Fori(0, IMAGES - 1) as i:
                image0(i, False)
            image0(IMAGES - 1, True)

            def values_high(plan, name):
                v = int(name[-1])
                wait_acc(plan.number(name))
                for j in range(2):
                    ins = nc.scalar.activation(
                        v_st[:, 2 * v + j, :, 0, :],
                        acc[:, plan.bank(name), j * C:(j + 1) * C].rearrange("p (h d) -> p h d", d=HD), ACT.Copy)
                ins.then_inc(acc_high, 1)

            def output_rows(plan, name, i):
                j = int(name[-1])
                pair = (j // 2) % 2
                rows = slice((j % 2) * HD, (j % 2 + 1) * HD)
                wait_acc(plan.number(name))
                if j % 2 == 0:
                    act.wait_ge(o_split, FREE_CREDIT + 4 * i + max(j // 2 - 1, 0))
                nc.scalar.activation(o_sum[rows, pair, :], acc[HD:2 * HD, plan.bank(name), :], ACT.Identity,
                                     bias=vec[rows, BV + pair:BV + pair + 1], scale=1.0).then_inc(o_part, 1)

            def pair_high(plan, name, i):
                pair = (int(name[-1]) // 2) % 2
                act.wait_ge(acc_evac, EVAC_CREDIT + plan.number(name) + 1)
                nc.scalar.activation(o_hi[:, pair, :], o_sum[:, pair, :], ACT.Copy).then_inc(o_high, 1)

            def pairs_of(plan, step, i):
                for name in image_groups(step):
                    if plan.has(name) and name in PAIR_ENDS:
                        pair_high(plan, name, i - 1 if name == "prev_av7" else i)

            def evacuate(plan, names, i):
                for name in names:
                    if not plan.has(name):
                        continue
                    if name.startswith("next_qk"):
                        chunk_high(plan, name, i + 1)
                    elif name.startswith(("qk", "first_qk")):
                        chunk_high(plan, name, i)
                    elif name.startswith("v"):
                        values_high(plan, name)
                    elif name == "prev_av7":
                        output_rows(plan, name, i - 1)
                    elif name.startswith("av"):
                        output_rows(plan, name, i)

            for t in range(LAG):
                exp(T1_BASE, t)

            def image1(i):
                plan, t1 = plan1(i), T1_BASE + T1_IMAGE * i
                for s in range(T1_IMAGE):
                    j = s // 4
                    if j >= 2:
                        before = plan.number(f"av{j - 2}")
                    elif plan.first:
                        before = None
                    elif j == 1:
                        before = plan.number("prev_av7")
                    else:
                        before = plan.base - (LAYER1[::-1].index("av6") + 1)
                    if s >= SUM_BEHIND:
                        evacuate(plan, head_outputs(STEPS1[s - SUM_BEHIND]), i)
                    trans_high(t1, s, before)
                    if s + LAG < T1_IMAGE or not plan.last:
                        exp(t1, s + LAG)
                    if not plan.last and s - 1 in NORM_STEPS1:
                        norm_chunk_high(i + 1, NORM_STEPS1.index(s - 1))
                    if s >= PAIR_BEHIND:
                        pairs_of(plan, STEPS1[s - PAIR_BEHIND], i)
                    evacuate(plan, other_groups(STEPS1[s]), i)
                evacuate(plan, head_outputs(STEPS1[T1_IMAGE - 1]), i)

            image1(0)
            with act.Fori(1, IMAGES - 1) as i:
                image1(i)
            image1(IMAGES - 1)
            evacuate(PLAN_EPILOGUE, image_groups(STEP_EPILOGUE), IMAGES)
            pairs_of(PLAN_EPILOGUE, STEP_EPILOGUE, IMAGES)

        @block.vector
        def _(dve):
            dve.sem_inc(acc_evac, EVAC_CREDIT)
            dve.sem_inc(xT_split, FREE_CREDIT)
            dve.sem_inc(pt_split, SPLIT_CREDIT)

            def row_max(t0, t):
                dve.wait_ge(scores_ready, t0 + t + 1)
                nc.vector.tensor_reduce(negmax[:, t % 2:t % 2 + 1], scores[:, t % 2, :], AX_X, ALU.max,
                                        negate=True).then_inc(max_ready, 1)

            def recip(t0, t):
                dve.wait_ge(exp_ready, EXP_CREDIT + t0 + t + 1)
                nc.vector.reciprocal(rsum[:, t % 2:t % 2 + 1], rowsum[:, t % 2:t % 2 + 1]).then_inc(rsum_ready, 1)

            def trans_low(t0, t):
                for h in range(2):
                    dve.wait_ge(pt_high, 2 * (t0 + t) + h + 1)
                    slot = (t // 4) % 2
                    nc.vector.tensor_tensor(pt_block(pt_lo, slot, t, h),
                                            trans[:, h, :].rearrange("p (j n) -> p j n", n=P),
                                            pt_block(pt_hi, slot, t, h).bitcast(F32),
                                            ALU.subtract).then_inc(pt_split, 1)

            def wait_acc(number):
                dve.wait_ge(acc_done, GROUP_CREDIT + number + 1)

            links = [0]

            def link(instructions):
                for ins in instructions:
                    ins.then_inc(gn_chain, 1)
                links[0] += len(instructions)
                dve.wait_ge(gn_chain, links[0])

            def norm_channels(n):
                first, end = GN_SETS[n]
                for m in range(KT * first, KT * end):
                    nc.vector.bn_aggr(gn_mv[:, m // KT, m % KT, :], y_stats[:, m * 12:(m + 1) * 12])\
                        .then_inc(gn_stats, 1)

            def norm_deviations(n, plan, name="gn0"):
                images = slice(*GN_SETS[n])
                size = GN_SETS[n][1] - GN_SETS[n][0]
                avg = acc[:, plan.bank(name), 0:size * KT * 2].rearrange("p (i k v) -> p i k v", k=KT, v=2)
                wait_acc(plan.number(name))
                nc.vector.tensor_copy(gn_mean[:, images, :], avg[:, :, :, 0]).then_inc(gn_chain, 1)
                links[0] += 1
                nc.vector.tensor_copy(gn_var[:, images, :], avg[:, :, :, 1]).then_inc(acc_evac, 1)
                dve.wait_ge(gn_chain, links[0])
                link([nc.vector.tensor_tensor(gn_dev[:, images, :], gn_mv[:, images, :, 0], gn_mean[:, images, :],
                                              ALU.subtract)])
                nc.vector.tensor_tensor(gn_sqdev[:, images, :], gn_dev[:, images, :], gn_dev[:, images, :],
                                        ALU.mult).then_inc(gn_dev_ready, 1)

            def norm_variance(n, plan, name="gn1"):
                images = slice(*GN_SETS[n])
                size = GN_SETS[n][1] - GN_SETS[n][0]
                dev = acc[:, plan.bank(name), 0:size * KT].rearrange("p (i k) -> p i k", k=KT)
                wait_acc(plan.number(name))
                dve.wait_ge(acc_evac, EVAC_CREDIT + plan.number(name.replace("1", "0")) + 1)
                nc.vector.scalar_tensor_tensor(gn_var[:, images, :], dev, EPS, gn_var[:, images, :],
                                               ALU.add, ALU.add).then_inc(acc_evac, 1)
                dve.wait_ge(acc_evac, EVAC_CREDIT + plan.number(name) + 1)
                dve.sem_inc(gn_var_ready, 1)

            def norm_affine(n):
                first, end = GN_SETS[n]
                dve.wait_ge(gn_root_ready, n + 1)
                images = range(first, end)
                link([nc.vector.tensor_tensor(gn_scale[:, m, 0:KT], gn_root[:, m, :], vec[:, GNW:GNW + KT],
                                              ALU.mult) for m in images])
                link([nc.vector.tensor_tensor(gn_scale[:, m, KT:2 * KT], gn_mean[:, m, :],
                                              gn_scale[:, m, 0:KT], ALU.mult) for m in images])
                link([nc.vector.tensor_tensor(gn_scale[:, m, KT:2 * KT], vec[:, GNB:GNB + KT],
                                              gn_scale[:, m, KT:2 * KT], ALU.subtract) for m in images])

            def norm_next(m):
                nc.vector.tensor_copy(gn_now[:, :], gn_scale[:, m, :]).then_inc(gn_affine, 1)

            def weight_low(w):
                dve.wait_ge(w_high, WEIGHTS.index(w) + 1)
                nc.vector.scalar_tensor_tensor(flat(w_lo[w]), flat(w_raw[w]), QSCALE if w == "q" else 1.0,
                                               flat(w_hi[w]).bitcast(F32), ALU.mult, ALU.subtract).then_inc(w_split, 1)

            def x_part_low(i, half):
                dve.wait_ge(x_high, X_HALVES * i + half + 1)
                cols = slice(half * H, (half + 1) * H)
                nc.vector.tensor_tensor(x_lo[:, :, cols], x_raw[:, :, cols], x_hi[:, :, cols].bitcast(F32),
                                        ALU.subtract).then_inc(x_split, 1)

            def low(lo, hi, plan, name, highs):
                dve.wait_ge(acc_high, highs)
                nc.vector.tensor_tensor(lo, acc[:, plan.bank(name), :], hi.bitcast(F32),
                                        ALU.subtract).then_inc(acc_evac, 1)

            def a_low(plan, name, highs):
                a = int(name[-1])
                cols = slice((a // 2) * H, (a // 2 + 1) * H)
                low(a_lo[:, a % 2, cols], a_hi[:, a % 2, cols], plan, name, highs)

            weight_low("b")
            weight_low("c")
            x_part_low(0, 0)
            for ct in range(KT):
                dve.wait_ge(acc_high, ct + 1)
                nc.vector.tensor_tensor(wk_lo[:, ct, :], acc[:, ct, 0:C], wk_hi[:, ct, :].bitcast(F32),
                                        ALU.subtract).then_inc(acc_evac, 1)
            x_part_low(0, 1)
            for n, (name, w) in enumerate(zip(FIRST_A, LATER_WEIGHTS)):
                a_low(PLAN_FIRST_A, name, KT + n + 1)
                weight_low(w)
            weight_low(LATER_WEIGHTS[-1])
            dve.wait_ge(vec_loaded, 16)
            nc.vector.tensor_scalar(bq8[:, :], vec[:, BQ:BQ + 2], QSCALE, None, ALU.mult).then_inc(w_split, 1)

            HIGH0 = KT + len(FIRST_A)
            KINDS0, KINDS1 = ("a", "qk"), ("v", "qk")
            HIGH_IMAGE0 = plan0(0).until(LAYER0[-1], KINDS0)
            HIGH_LAYER0 = HIGH0 + HIGH_IMAGE0 * (IMAGES - 1) + plan0(IMAGES - 1, True).until(LAYER0_LAST[-1], KINDS0)
            HIGH_IMAGE1 = plan1(1).until(plan1(1).names[-1], KINDS1)

            def chunk_low(plan, name, highs):
                r = int(name[-1])
                dve.wait_ge(acc_high, highs)
                nc.vector.scalar_tensor_tensor(qk[:, r % 2, 1, :], acc[:, plan.bank(name), :], qk_bias(r),
                                               qk[:, r % 2, 0, :].bitcast(F32),
                                               ALU.add, ALU.subtract).then_inc(acc_evac, 1)

            def image0(i, last):
                plan, t0 = plan0(i, last), T0_IMAGE * i

                highs = HIGH0 + HIGH_IMAGE0 * i

                def result(a):
                    if a == 0:
                        dve.wait_ge(res_loaded, 64 * i + 64)
                    wait_acc(plan.number(f"y{a}"))
                    nc.vector.scalar_tensor_tensor(y_out[:, a, :], acc[:, plan.bank(f"y{a}"), :],
                                                   vec[:, GAMMA:GAMMA + 1], y_out[:, a, :],
                                                   ALU.mult, ALU.add).then_inc(acc_evac, 1)
                    dve.wait_ge(acc_evac, EVAC_CREDIT + plan.number(f"y{a}") + 1)
                    col = ((i * KT + a % 2) * 2 + a // 2) * 6
                    nc.vector.bn_stats(y_stats[:, bass.ds(col, 6)], y_out[:, a, :]).then_inc(y_ready, 1)

                if last:
                    dve.wait_ge(y_ready, 4 * (IMAGES - 1))
                    norm_channels(0)
                for s in range(T0_IMAGE):
                    if s >= 1:
                        recip(t0, s - 1)
                    row_max(t0, s)
                    if s >= LAG:
                        trans_low(t0, s - LAG)
                    if s in XT_STEPS:
                        dve.wait_ge(xT_high, XT_PARTS * i + XT_STEPS.index(s) + 1)
                        nc.vector.tensor_tensor(xT_part(xT_lo, s), xT_part(xT_raw, s),
                                                xT_part(xT_hi, s).bitcast(F32), ALU.subtract).then_inc(xT_split, 1)
                    if last and s == 0:
                        norm_deviations(0, plan)
                    if last and s == 1:
                        norm_variance(0, plan)
                    if last and s == 2:
                        norm_affine(0)
                        norm_next(0)
                recip(t0, T0_IMAGE - 1)
                for name in TAIL0_LAST if last else TAIL0:
                    n = int(name[-1])
                    if name.startswith("t"):
                        trans_low(t0, n)
                    elif name.startswith("av"):
                        low(u_lo[:, n % 2, :], u_hi[:, n % 2, :], plan, name, highs + plan.until(name, KINDS0))
                    elif name.startswith("y"):
                        result(n)
                        if name == "y1" and not last:
                            for half in range(X_HALVES):
                                x_part_low(i + 1, half)
                    elif name.startswith("next_a"):
                        a_low(plan, name, highs + plan.until(name, KINDS0))
                    else:
                        chunk_low(plan, name, highs + plan.until(name, KINDS0))

            with dve.Fori(0, IMAGES - 1) as i:
                image0(i, False)
            image0(IMAGES - 1, True)
            dve.wait_ge(y_ready, 4 * IMAGES)
            norm_channels(1)

            def values_low(plan, name, highs):
                v = int(name[-1])
                dve.wait_ge(acc_high, highs)
                for j in range(2):
                    ins = nc.vector.tensor_tensor(
                        v_st[:, 2 * v + j, :, 1, :],
                        acc[:, plan.bank(name), j * C:(j + 1) * C].rearrange("p (h d) -> p h d", d=HD),
                        v_st[:, 2 * v + j, :, 0, :].bitcast(F32), ALU.subtract)
                ins.then_inc(acc_evac, 1)

            def output_add(plan, name, i):
                j = int(name[-1])
                pair = (j // 2) % 2
                rows = slice((j % 2) * HD, (j % 2 + 1) * HD)
                dve.wait_ge(o_part, 8 * i + j + 1)
                nc.vector.tensor_tensor(o_sum[rows, pair, :], acc[0:HD, plan.bank(name), :],
                                        o_sum[rows, pair, :], ALU.add).then_inc(acc_evac, 1)

            def result(plan, name, i):
                n = int(name[-1])
                o = n % 2
                wait_acc(plan.number(name))
                dve.wait_ge(yres_loaded, 64 * i + 32 * (n // 2) + 32)
                nc.vector.scalar_tensor_tensor(y_res[:, o, :], acc[:, plan.bank(name), :],
                                               vec[:, BP + o:BP + o + 1], y_res[:, o, :],
                                               ALU.add, ALU.add).then_inc(acc_evac, 1)

            def evacuate(plan, names, i, highs_before):
                for name in names:
                    if not plan.has(name):
                        continue
                    highs = highs_before + plan.until(name, KINDS1)
                    if name == "first_gn0":
                        norm_deviations(1, plan, name)
                    elif name == "first_gn1":
                        norm_variance(1, plan, name)
                    elif "qk" in name:
                        chunk_low(plan, name, highs)
                    elif name.startswith("v"):
                        values_low(plan, name, highs)
                    elif name == "prev_av7":
                        output_add(plan, name, i - 1)
                    elif name.startswith("av"):
                        output_add(plan, name, i)
                    elif name.startswith("prev_out"):
                        result(plan, name, i - 1)
                    else:
                        result(plan, name, i)

            row_max(T1_BASE, 0)
            recip(T1_BASE, 0)
            row_max(T1_BASE, 1)

            def image1(i):
                plan, t1 = plan1(i), T1_BASE + T1_IMAGE * i
                highs = HIGH_LAYER0 + (0 if plan.first else 1 + HIGH_IMAGE1 * i)
                for s in range(T1_IMAGE):
                    if s + 1 < T1_IMAGE or not plan.last:
                        recip(t1, s + 1)
                    if s + LAG < T1_IMAGE or not plan.last:
                        row_max(t1, s + LAG)
                    trans_low(t1, s)
                    if s >= SUM_BEHIND:
                        evacuate(plan, head_outputs(STEPS1[s - SUM_BEHIND]), i, highs)
                    if s == 1 and not plan.last:
                        dve.wait_ge(h_split, 4 * i + 4)
                        norm_next(i + 1)
                    if s == 18 and plan.first:
                        norm_affine(1)
                    evacuate(plan, other_groups(STEPS1[s]), i, highs)
                evacuate(plan, head_outputs(STEPS1[T1_IMAGE - 1]), i, highs)

            image1(0)
            with dve.Fori(1, IMAGES - 1) as i:
                image1(i)
            image1(IMAGES - 1)
            output_add(PLAN_EPILOGUE, "prev_av7", IMAGES - 1)
            dve.wait_ge(o_high, 4 * IMAGES)
            pair_difference(nc.vector, 1)
            evacuate(PLAN_EPILOGUE, ["prev_out2", "prev_out3"], IMAGES, 0)

        @block.tensor
        def _(pe):
            pe.sem_inc(transposed, TRANS_CREDIT)
            pe.sem_inc(acc_done, GROUP_CREDIT)

            def run(dst, pairs, starts=True, stops=True):
                for n, (w, m) in enumerate(pairs):
                    ins = nc.tensor.matmul(dst, w, m, start=(starts and n == 0),
                                           stop=(stops and n == len(pairs) - 1))
                return ins

            def bank_free(plan, name):
                pe.wait_ge(acc_evac, EVAC_CREDIT + plan.before(name) + 1)

            def group(plan, name, pairs, cols=slice(0, H), part=0, parts=1):
                if part == 0:
                    bank_free(plan, name)
                size = len(pairs) // parts
                ins = run(acc[:, plan.bank(name), cols], pairs[part * size:(part + 1) * size],
                          part == 0, part == parts - 1)
                if part == parts - 1:
                    ins.then_inc(acc_done, 1)

            def evacuated(number):
                pe.wait_ge(acc_evac, EVAC_CREDIT + number + 1)

            def over_k(w, m):
                return [pair for k in range(KT)
                        for pair in products((w(0, k), m(0, k)), (w(1, k), m(1, k)))]

            def transpose_tile(t0, t):
                pe.wait_ge(prob_ready, t0 + t + 1)
                for h in range(2):
                    pe.wait_ge(pt_split, 2 * (t0 + t) + h + 1)
                    for b in range(4):
                        j = 4 * h + b
                        ins = nc.tensor.transpose(trans[:, h, b * P:(b + 1) * P],
                                                  prob[:, t % 2, j * P:(j + 1) * P], ident[:, :])
                    ins.then_inc(transposed, 1)

            w = lambda name: (lambda part, k, cols: (w_hi, w_lo)[part][name][:, k, cols])
            wb, wc, wd, wq, wk, wv, wp = (w(n) for n in "bcdqkvp")
            abc = lambda part, k, cols: (wk_hi, wk_lo)[part][:, k, cols]
            col = lambda n, size: slice(n * size, (n + 1) * size)

            pe.wait_ge(w_split, 2)
            for ct in range(KT):
                run(acc[:, ct, 0:C], over_k(lambda part, k: wb(part, k, col(ct, P)),
                                            lambda part, k: wc(part, k, slice(0, C)))).then_inc(acc_done, 1)
            pe.wait_ge(consts_ready, 6)
            evacuated(1)

            def a_group(plan, name):
                a = int(name[-1])
                group(plan, name, over_k(lambda part, k: abc(part, k, col(a % 2, P)),
                                         lambda part, k: (x_hi, x_lo)[part][:, k, col(a // 2, H)]))

            for n, name in enumerate(FIRST_A):
                if n % 2 == 0:
                    pe.wait_ge(x_split, n // 2 + 1)
                a_group(PLAN_FIRST_A, name)

            h_part = lambda part, k, cols: (h_hi, h_lo)[part][:, k, cols]

            def chunk(plan, name, part=0, parts=1):
                r = int(name[-1])
                wt = wk if r % 4 >= 2 else wq
                group(plan, name, over_k(lambda part, k: wt(part, k, col(r // 4, P)),
                                         lambda part, k: h_part(part, k, col(r % 2, H))),
                      part=part, parts=parts)

            def norm_group(plan, name, n, src, width):
                first, end = GN_SETS[n]
                rhs = src[:, first:end].rearrange("p i k v -> p (i k v)" if width == 2 else "p i k -> p (i k)")
                group(plan, name, [(gavg[:, :], rhs)], slice(0, (end - first) * KT * width))

            def image0(i, last):
                plan, t0 = plan0(i, last), T0_IMAGE * i

                def scores0(s):
                    pe.wait_ge(exp_ready, t0 + s + 1)
                    for mh in range(2):
                        ins = run(scores[:, s % 2, col(mh, H)],
                                  over_k(lambda part, k: (a_hi, a_lo)[part][:, k, col(s, P)],
                                         lambda part, k: (x_hi, x_lo)[part][:, k, col(mh, H)]))
                    ins.then_inc(scores_ready, 1)

                def values(n):
                    half, ct = n // 2, n % 2
                    if ct == 0:
                        pe.wait_ge(pt_split, SPLIT_CREDIT + 2 * t0 + 8 * (half + 1))
                    group(plan, f"av{n}", [
                        pair for j in range(NT)
                        for pair in products((xT_hi[:, j, col(ct, P)], pt_hi[:, half, j, :]),
                                             (xT_lo[:, j, col(ct, P)], pt_lo[:, half, j, :]))])

                def result(n):
                    if n % 2 == 0:
                        evacuated(plan.number(f"av{n + 1}"))
                    if n == 0:
                        pe.wait_ge(w_split, len(WEIGHTS) + 1)
                    group(plan, f"y{n}", over_k(
                        lambda part, k: wd(part, k, col(n % 2, P)),
                        lambda part, k: (u_hi, u_lo)[part][:, k, :]))

                for s in range(T0_IMAGE):
                    if s == 0:
                        evacuated(plan.base - 3)
                    if s == 4:
                        evacuated(plan.base - 1)
                    scores0(s)
                    if last and s == 0:
                        pe.wait_ge(gn_stats, KT * GN_SETS[0][1])
                        norm_group(plan, "gn0", 0, gn_mv, 2)
                    if last and s == 1:
                        pe.wait_ge(gn_dev_ready, 1)
                        norm_group(plan, "gn1", 0, gn_sqdev, 1)
                    if s >= LAG:
                        transpose_tile(t0, s - LAG)
                pe.wait_ge(xT_split, FREE_CREDIT + XT_PARTS * (i + 1))
                for name in TAIL0_LAST if last else TAIL0:
                    n = int(name[-1])
                    if name.startswith("t"):
                        transpose_tile(t0, n)
                    elif name.startswith("av"):
                        values(n)
                    elif name.startswith("y"):
                        result(n)
                    elif name.startswith("next_a"):
                        if n == 0:
                            pe.wait_ge(x_split, X_HALVES * (i + 2))
                        a_group(plan, name)
                    else:
                        if n == 0:
                            pe.wait_ge(h_split, 4)
                        chunk(plan, name)

            with pe.Fori(0, IMAGES - 1) as i:
                image0(i, False)
            image0(IMAGES - 1, True)

            def project_v(plan, name):
                v = int(name[-1])
                bank_free(plan, name)
                for j in range(2):
                    ins = run(acc[:, plan.bank(name), col(j, C)],
                              over_k(lambda part, k: h_part(part, k, col(2 * v + j, P)),
                                     lambda part, k: wv(part, k, slice(0, C))))
                ins.then_inc(acc_done, 1)

            def values(plan, name, part, parts, t1):
                j = int(name[-1])
                if part == 0:
                    pe.wait_ge(pt_split, SPLIT_CREDIT + 2 * t1 + 8 * (j + 1))
                if name == "av0":
                    evacuated(plan.number(f"v{part}"))
                group(plan, name, [(v_st[:, b, j % 4, :, :].rearrange("p v d -> p (v d)"), src[:, j % 2, b, :])
                                   for b in range(NT) for src in (pt_hi, pt_lo)], part=part, parts=parts)

            def project_out(plan, name, i, part, parts):
                n = int(name[-1])
                if n % 2 == 0:
                    pe.wait_ge(o_split, FREE_CREDIT + 4 * i + n + (1 if part + 1 < parts else 2))
                group(plan, name, over_k(lambda part, k: wp(part, k, col(n % 2, P)),
                                         lambda part, k: (o_hi, o_lo)[part][:, k, :]), part=part, parts=parts)

            def run_groups(plan, step, i, t1):
                for g in step:
                    name, part, parts = g if not isinstance(g, str) else (g, 0, 1)
                    if not plan.has(name):
                        continue
                    if name == "next_qk0":
                        pe.wait_ge(h_split, 4 * i + 8)
                    if name == "first_gn0":
                        pe.wait_ge(gn_stats, KT * IMAGES)
                        norm_group(plan, name, 1, gn_mv, 2)
                    elif name == "first_gn1":
                        pe.wait_ge(gn_dev_ready, 2)
                        norm_group(plan, name, 1, gn_sqdev, 1)
                    elif "qk" in name:
                        chunk(plan, name, part, parts)
                    elif name == "prev_av7":
                        values(plan, name, part, parts, t1 - T1_IMAGE)
                    elif name.startswith("av"):
                        values(plan, name, part, parts, t1)
                    elif name.startswith("v"):
                        project_v(plan, name)
                    elif name.startswith("prev_out"):
                        project_out(plan, name, i - 1, part, parts)
                    else:
                        project_out(plan, name, i, part, parts)

            def scores1(i, t1, s):
                head, tile = (s // 4) % 4, 4 * (s // 16) + s % 4
                if s in (0, 8):
                    for slot in range(2):
                        pe.wait_ge(qk_stacked[slot], FREE_CREDIT + QK_IMAGE * i + CHUNK_DMA * (2 if s == 0 else 4))
                pe.wait_ge(exp_ready, t1 + s + 1)
                for mh in range(2):
                    ins = run(scores[:, s % 2, col(mh, H)],
                              [(q_st[:, head, col(tile, P)], k_st[:, part, head, col(mh, H)]) for part in range(2)])
                ins.then_inc(scores_ready, 1)

            for t in range(LAG):
                scores1(0, T1_BASE, t)

            def image1(i):
                plan, t1 = plan1(i), T1_BASE + T1_IMAGE * i
                for s in range(T1_IMAGE):
                    if plan.first and s == 0:
                        run_groups(plan, STEPS1[s], i, t1)
                    if s + LAG < T1_IMAGE:
                        scores1(i, t1, s + LAG)
                    elif not plan.last:
                        scores1(i + 1, t1 + T1_IMAGE, s + LAG - T1_IMAGE)
                    transpose_tile(t1, s)
                    if not (plan.first and s == 0):
                        run_groups(plan, STEPS1[s], i, t1)

            image1(0)
            with pe.Fori(1, IMAGES - 1) as i:
                image1(i)
            image1(IMAGES - 1)
            run_groups(PLAN_EPILOGUE, STEP_EPILOGUE, IMAGES, T1_BASE + T1_IMAGE * IMAGES)


_IN = {"x": "x", "b": "L0_conv_Wb", "c": "L0_conv_Wc", "d": "L0_conv_Wd", "q": "L1_conv_wq",
       "k": "L1_conv_wk", "v": "L1_conv_wv", "p": "L1_conv_wp"}


def kernel(**inputs):
    import numpy as np
    import concourse.bacc as bacc
    from concourse.bass_utils import run_bass_kernel_spmd

    x = np.ascontiguousarray(inputs["x"])
    arrays = {
        "in_x": x.reshape(IMAGES, KT, P, N),
        "in_xT": np.ascontiguousarray(x.reshape(IMAGES, C, N).transpose(0, 2, 1)),
    }
    for w in "bc":
        arrays[f"in_w{w}"] = np.ascontiguousarray(inputs[_IN[w]])
    arrays["in_wlater"] = np.ascontiguousarray(
        np.stack([np.asarray(inputs[_IN[w]]).T for w in LATER_WEIGHTS]).reshape(-1, P, C))
    columns = [np.asarray(inputs[n]).reshape(KT, P).T for n in (
        "L1_conv_bq", "L1_conv_bk", "L1_conv_bv", "L1_conv_bp", "L1_conv_gamma", "L1_conv_beta")]
    columns.append(np.broadcast_to(np.asarray(inputs["L0_conv_gamma"]).reshape(1, 1), (P, 1)))
    arrays["in_vecs"] = np.ascontiguousarray(np.concatenate(columns, axis=1))

    nc = bacc.Bacc("TRN2", target_bir_lowering=False, num_devices=1)
    t = {n: nc.dram_tensor(n, a.shape, F32, kind="ExternalInput").ap() for n, a in arrays.items()}
    out = nc.dram_tensor("out_0", (IMAGES, KT, P, N), F32, kind="ExternalOutput").ap()
    build(nc, t["in_x"], t["in_xT"], {w: t[f"in_w{w}"] for w in ("b", "c", "later")}, t["in_vecs"], out)
    r = run_bass_kernel_spmd(nc, [arrays], core_ids=[0])
    return r.results[0]["out_0"].reshape(IMAGES, C, 32, 32)
```

```python
from contextlib import ExitStack

import concourse.bass as bass
from concourse import mybir

F32 = mybir.dt.float32
F32R = mybir.dt.float32r
ALU = mybir.AluOpType
ACT = mybir.ActivationFunctionType
AX_X = mybir.AxisListType.X

P = 128
IMAGES = 4
C = 256
KT = C // P
N = 1024
H = 512
NT = N // P
HEADS = 4
HD = C // HEADS
GROUP = C // 32
EPS = 1e-5
NORM_ROOT_STEP = 17
NORM_AFFINE_STEP = 18
QSCALE = HD ** -0.5

T0_IMAGE = NT
T1_IMAGE = HEADS * NT
T1_BASE = IMAGES * T0_IMAGE
LAG = 2

FIRST_A = ["a0", "a1", "a2", "a3"]
D_STEPS = [1, 2, 4, 5]
TAIL0 = ["av0", "t6", ("av1", 0, 2), "t7", ("av1", 1, 2), "av2", "next_a0", ("av3", 0, 3), "next_a1",
         ("av3", 1, 3), "next_a2", ("av3", 2, 3), "next_a3"]
TAIL0_LAST = ["av0", "t6", "next_qk0", ("av1", 0, 2), "t7", ("av1", 1, 2), "next_qk1", ("av2", 0, 2),
              "next_qk2", ("av2", 1, 2), "next_qk3", ("av3", 0, 2), "next_qk4", ("av3", 1, 2),
              "s0", "next_qk5", "s1"]
TILES0 = ("t6", "t7", "s0", "s1")


def ends(parts):
    return [g if isinstance(g, str) else g[0] for g in parts if isinstance(g, str) or g[1] == g[2] - 1]


D_GROUPS = ["d0", "d1", "d2", "d3"]
PARTS0 = D_GROUPS + [g for g in TAIL0 if g not in TILES0]
PARTS0_LAST = ["gn0", "gn1"] + D_GROUPS + [g for g in TAIL0_LAST if g not in TILES0]
LAYER0 = ends(PARTS0)

STEPS1 = {
    0: ["first_qk6"], 1: ["qk7"], 2: ["v0"], 3: ["v1"], 5: ["v2"], 6: ["v3"],
    7: ["prev_out2"], 9: [("prev_out3", 0, 3)], 10: [("prev_out3", 1, 3)],
    11: [("prev_out3", 2, 3)], 13: ["first_gn0"], 15: ["first_gn1"],
    21: ["next_qk0"], 22: ["out0"], 23: ["next_qk1"], 25: ["next_qk2"], 26: ["next_qk3"],
    27: ["out1"], 29: ["next_qk4"], 30: ["next_qk5"], 31: ["next_qk6"],
}
AV_PARTS = 4
for step in range(T1_IMAGE):
    head_half = (step // AV_PARTS - 1) % 8
    av = ("prev_" if step < AV_PARTS else "") + f"av{head_half}"
    STEPS1.setdefault(step, []).append((av, step % AV_PARTS, AV_PARTS))
PARTS1 = [g for step in range(T1_IMAGE) for g in STEPS1[step]]
LAYER1 = ends(PARTS1)
PAIR_ENDS = ["prev_av7", "av1", "av3", "av5"]
SUM_BEHIND, PAIR_BEHIND = 1, 2
DVE_TILES = 1
EPILOGUE_AV, EPILOGUE_OUT = ["left_av", "right_av"], ["left_out", "right_out"]
SIDE = H // 2
NORM_STEPS0 = [3, 4, 5, 6]
NORM_STEPS1 = [7, 10, 14, 17]
X_HALVES = 2


def of_image(parts, first=False, last=False):
    def has(name):
        return not ((first and name.startswith("prev_")) or (last and name.startswith("next_"))
                    or (not first and name.startswith("first_")))
    return [g for g in parts if has(g if isinstance(g, str) else g[0])]


STRETCHES = {"first_a": (FIRST_A, 1), "layer0": (PARTS0, IMAGES - 1), "layer0_last": (PARTS0_LAST, 1),
             "layer1_first": (of_image(PARTS1, first=True), 1), "layer1": (of_image(PARTS1), IMAGES - 2),
             "layer1_last": (of_image(PARTS1, last=True), 1), "epilogue": (EPILOGUE_AV + EPILOGUE_OUT, 1)}


def place_groups():
    last_in = {0: 0, 1: 1}
    places, bases, base = {}, {}, KT
    for stretch, (parts, times) in STRETCHES.items():
        names = ends(parts)
        for _ in range(times):
            running, place = {}, {}
            for g in parts:
                name, part, of = (g, 0, 1) if isinstance(g, str) else g
                if part == 0:
                    bank = min((b for b in last_in if b not in running.values()), key=last_in.get)
                    running[name], place[name] = bank, (bank, last_in[bank] - base)
                if part == of - 1:
                    last_in[running.pop(name)] = base + names.index(name)
            assert places.setdefault(stretch, place) == place
            bases.setdefault(stretch, base)
            base += len(names)
    return places, bases


PLACES, BASES = place_groups()


class Plan:

    def __init__(self, stretch, repeat=0):
        self.names = ends(STRETCHES[stretch][0])
        self.places = PLACES[stretch]
        self.base = BASES[stretch] + len(self.names) * repeat
        self.first, self.last = stretch == "layer1_first", stretch == "layer1_last"

    def has(self, name):
        return name in self.names

    def number(self, name):
        return self.base + self.names.index(name)

    def bank(self, name):
        return self.places[name][0]

    def before(self, name):
        return self.base + self.places[name][1]

    def until(self, name, kinds):
        return sum(n.removeprefix("prev_").removeprefix("next_").removeprefix("first_").startswith(kinds)
                   for n in self.names[:self.names.index(name) + 1])


def plan0(i, last=False):
    return Plan("layer0_last") if last else Plan("layer0", i)


def plan1(i):
    if isinstance(i, int) and i == 0:
        return Plan("layer1_first")
    if isinstance(i, int) and i == IMAGES - 1:
        return Plan("layer1_last")
    return Plan("layer1", i - 1)


EXP_CREDIT = 2
TRANS_CREDIT = 4
SPLIT_CREDIT = 2
GROUP_CREDIT = 6
EVAC_CREDIT = 2

FREE_CREDIT = 1

BQ, BK, BV, BP, GNW, GNB, GAMMA = 0, 2, 4, 6, 8, 10, 12
NVEC = 13
GN_SETS = [(0, IMAGES - 1), (IMAGES - 1, IMAGES)]
WEIGHTS = ["b", "c", "d", "q", "k", "v", "p"]
LATER_WEIGHTS = WEIGHTS[2:]


def products(his, los):
    (ah, bh), (al, bl) = his, los
    return [(ah, bh), (al, bh), (ah, bl)]


def build(nc, x, weights, vecs, out):
    y_dram = nc.dram_tensor("y_scratch", (IMAGES, KT, P, N), F32, kind="Internal").ap()
    ctx = ExitStack()
    with ctx:
        def sb(name, shape, dt=F32, scope=ctx):
            return scope.enter_context(nc.sbuf_tensor(name, shape, dt))

        def sem(name):
            return ctx.enter_context(nc.semaphore(name))

        vec = sb("vec", [P, NVEC])
        bq8 = sb("bq8", [P, 2])
        ident = sb("ident", [P, P])
        gavg = sb("gavg", [P, P])
        gn_mv = sb("gn_mv", [P, IMAGES, KT, 2])
        gn_mean = sb("gn_mean", [P, IMAGES, KT])
        gn_var = sb("gn_var", [P, IMAGES, KT])
        gn_root = sb("gn_root", [P, IMAGES, KT])
        gn_dev = sb("gn_dev", [P, IMAGES, KT])
        gn_sqdev = sb("gn_sqdev", [P, IMAGES, KT])
        minus_half = sb("minus_half", [P, IMAGES, KT])
        gn_scale = sb("gn_scale", [P, IMAGES, 2 * KT])
        gn_now = sb("gn_now", [P, 2 * KT])
        y_stats = sb("y_stats", [P, IMAGES * KT * 2 * 6])
        negmax = sb("negmax", [P, 2])
        rowsum = sb("rowsum", [P, 2])
        rsum = sb("rsum", [P, 2])
        w_hi = {w: sb(f"w{w}_hi", [P, KT, C], F32R) for w in "dqkvp"}
        w_lo = {w: sb(f"w{w}_lo", [P, KT, C], F32R) for w in "dqkvp"}
        start = ExitStack()
        w_raw = {w: sb(f"w{w}_raw", [P, KT, C], F32, start) for w in "bc"}
        w_later = sb("w_later", [P, len(LATER_WEIGHTS), KT, C], F32, start)
        w_raw.update({w: w_later[:, n, :, :] for n, w in enumerate(LATER_WEIGHTS)})
        bc_hi = {w: sb(f"w{w}_hi", [P, KT, C], F32R, start) for w in "bc"}
        bc_lo = {w: sb(f"w{w}_lo", [P, KT, C], F32R, start) for w in "bc"}
        start.close()
        w_hi.update(bc_hi)
        w_lo.update(bc_lo)
        pt_hi = sb("pt_hi", [P, 2, NT, H], F32R)
        pt_lo = sb("pt_lo", [P, 2, NT, H], F32R)
        prob = sb("prob", [P, 2, N])
        h_hi = sb("h_hi", [P, KT, N], F32R)
        h_lo = sb("h_lo", [P, KT, N], F32R)
        y_in = sb("y_in", [P, KT, 2, H])

        layer0 = ExitStack()
        a_hi = sb("a_hi", [P, KT, N], F32R, layer0)
        a_lo = sb("a_lo", [P, KT, N], F32R, layer0)
        x_raw = sb("x_raw", [P, KT, N], F32, layer0)
        x_hi = sb("x_hi", [P, KT, N], F32R, layer0)
        x_lo = sb("x_lo", [P, KT, N], F32R, layer0)
        wk_hi = sb("wbc_hi", [P, KT, C], F32R, layer0)
        wk_lo = sb("wbc_lo", [P, KT, C], F32R, layer0)
        sb("unused", [P, 3 * N], F32, layer0)
        d_hi = sb("d_hi", [P, NT, C], F32R, layer0)
        d_lo = sb("d_lo", [P, NT, C], F32R, layer0)
        y_out = sb("y_out", [P, 4, H], F32, layer0)
        layer0.close()

        q_st = sb("q_st", [P, HEADS, N], F32R)
        k_st = sb("k_st", [P, 2, HEADS, N], F32R)
        qk = sb("qk", [P, 2, 2, H], F32R)
        v_st = sb("v_st", [P, NT, HEADS, 2, HD], F32R)
        o_sum = sb("o_sum", [P, 2, H])
        o_hi = sb("o_hi", [P, KT, H], F32R)
        o_lo = sb("o_lo", [P, KT, H], F32R)
        y_res = sb("y_res", [P, 2, H])

        scores = ctx.enter_context(nc.psum_tensor("scores", [P, 2, N], F32))
        trans = ctx.enter_context(nc.psum_tensor("trans", [P, 2, H], F32))
        acc = ctx.enter_context(nc.psum_tensor("acc", [P, 2, H], F32))

        consts_ready = sem("consts_ready")
        vec_loaded = sem("vec_loaded")
        w_loaded = sem("w_loaded")
        later_loaded = sem("later_loaded")
        w_high = sem("w_high")
        w_split = sem("w_split")
        x_loaded = [sem("x_loaded0"), sem("x_loaded1")]
        x_high = sem("x_high")
        x_split = sem("x_split")
        res_loaded = sem("res_loaded")
        y_ready = sem("y_ready")
        y_stored = sem("y_stored")
        scores_ready = sem("scores_ready")
        max_ready = sem("max_ready")
        exp_ready = sem("exp_ready")
        rsum_ready = sem("rsum_ready")
        prob_ready = sem("prob_ready")
        last_prob_ready = sem("last_prob_ready")
        transposed = sem("transposed")
        pt_high = sem("pt_high")
        pt_split = sem("pt_split")
        acc_done = sem("acc_done")
        acc_high = sem("acc_high")
        acc_evac = sem("acc_evac")
        gn_chain = sem("gn_chain")
        gn_var_ready = sem("gn_var_ready")
        gn_root_ready = sem("gn_root_ready")
        gn_stats = sem("gn_stats")
        gn_dev_ready = sem("gn_dev_ready")
        gn_affine = sem("gn_affine")
        y_loaded = sem("y_loaded")
        h_full = sem("h_full")
        h_high = sem("h_high")
        h_split = sem("h_split")
        qk_stacked = [sem("qk_stacked0"), sem("qk_stacked1")]
        o_part = sem("o_part")
        o_high = sem("o_high")
        o_split = sem("o_split")
        side_split = sem("side_split")
        yres_loaded = sem("yres_loaded")
        out_stored = sem("out_stored")
        pool_steps = sem("pool_steps")

        plan_first_a, plan_epilogue = Plan("first_a"), Plan("epilogue")
        CHUNK_DMA = 4 * 16
        QK_IMAGE = 4 * CHUNK_DMA

        def head_outputs(step):
            return [name for name in ends(step) if "av" in name]

        def other_groups(step):
            return [name for name in ends(step) if "av" not in name]

        def h_difference(engine, c):
            k, half = c // 2, c % 2
            cols = slice(half * H, (half + 1) * H)
            engine.tensor_tensor(h_lo[:, k, cols], y_in[:, k, half, :], h_hi[:, k, cols].bitcast(F32),
                                 ALU.subtract).then_inc(h_split, 1)

        def pair_difference(engine, pair):
            engine.tensor_tensor(o_lo[:, pair, :], o_sum[:, pair, :], o_hi[:, pair, :].bitcast(F32),
                                 ALU.subtract).then_inc(o_split, 1)

        def flat(ap):
            return ap.rearrange("p a b -> p (a b)")

        def pt_block(buf, half_slot, t, h):
            return buf[:, half_slot, 4 * h:4 * h + 4, (t % 4) * P:(t % 4 + 1) * P]

        def d_part(buf, n):
            return buf[:, 2 * n:2 * n + 2, :].rearrange("p a b -> p (a b)")

        def qk_bias(r):
            return vec[:, BK + r // 4:BK + r // 4 + 1] if r % 4 >= 2 else bq8[:, r // 4:r // 4 + 1]

        block = ctx.enter_context(nc.Block())

        @block.sync
        def _(sp):
            for s in (y_stored, out_stored, *qk_stacked):
                sp.sem_inc(s, FREE_CREDIT)
            for w in "bc":
                sp.dma_start(w_raw[w][:, :, :], weights[w].rearrange("(k p) c -> p k c", p=P)).then_inc(w_loaded, 16)

            def load_x(i):
                for half in range(X_HALVES):
                    cols = slice(half * H, (half + 1) * H)
                    sp.dma_start(x_raw[:, :, cols], x[i, :, :, cols].rearrange("k p n -> p k n")).then_inc(x_loaded[half], 16)

            load_x(0)
            sp.dma_start(vec[:, :], vecs).then_inc(vec_loaded, 16)
            sp.dma_start(w_later[:, :, :, :].rearrange("p w k c -> p (w k) c"),
                         weights["later"].rearrange("w p c -> p w c")).then_inc(later_loaded, 16)

            def evacuated(plan, name):
                sp.wait_ge(acc_evac, EVAC_CREDIT + plan.number(name) + 1)

            def restack(plan, name):
                r = int(name[-1])
                pair, is_k, half, slot = r // 4, r % 4 >= 2, r % 2, r % 2
                cols = slice(half * H, (half + 1) * H)
                evacuated(plan, name)
                for n in range(2):
                    head, rows = 2 * pair + n, slice(n * HD, (n + 1) * HD)
                    for u in range(2):
                        if is_k:
                            dst, src = k_st[u * HD:(u + 1) * HD, :, head, cols], qk[rows, slot, :, :]
                        else:
                            dst, src = q_st[u * HD:(u + 1) * HD, head, cols], qk[rows, slot, u, :]
                        sp.dma_start(dst.bitcast(F32), src.bitcast(F32)).then_inc(qk_stacked[slot], 16)

            def load_y(i):
                sp.dma_start(y_in[:, :, :, :], y_dram[i].rearrange("k p (a n) -> p k a n", a=2)).then_inc(y_loaded, 16)

            def image0(i, last):
                plan = plan0(i, last)
                sp.wait_ge(y_stored, FREE_CREDIT + i * 64)
                for a in range(4):
                    sp.dma_start(y_out[:, a, :], x[i, a % 2, :, (a // 2) * H:(a // 2 + 1) * H]).then_inc(res_loaded, 16)
                if last:
                    load_y(0)
                else:
                    sp.wait_ge(x_split, X_HALVES * (i + 1))
                    load_x(i + 1)
                for name in plan.names:
                    if name.startswith("next_qk"):
                        restack(plan, name)
                    elif name.startswith("av"):
                        a = int(name[-1])
                        sp.wait_ge(y_ready, 4 * i + a + 1)
                        sp.dma_start(y_dram[i, a % 2, :, (a // 2) * H:(a // 2 + 1) * H], y_out[:, a, :])\
                            .then_inc(y_stored, 16)

            with sp.Fori(0, IMAGES - 1) as i:
                image0(i, False)
            image0(IMAGES - 1, True)

            def load_residual(i, half):
                sp.wait_ge(out_stored, FREE_CREDIT + 64 * i + 32 * half)
                for o in range(2):
                    sp.dma_start(y_res[:, o, :], y_dram[i, o, :, half * H:(half + 1) * H]).then_inc(yres_loaded, 16)

            def store(plan, name, i):
                n = int(name[-1])
                evacuated(plan, name)
                sp.dma_start(out[i, n % 2, :, (n // 2) * H:(n // 2 + 1) * H], y_res[:, n % 2, :]).then_inc(out_stored, 16)

            def image1(i):
                plan = plan1(i)
                if plan.first:
                    restack(plan, "first_qk6")
                    sp.wait_ge(y_stored, FREE_CREDIT + IMAGES * 64)
                restack(plan, "qk7")
                if not plan.last:
                    sp.wait_ge(h_split, 4 * i + 4)
                    load_y(i + 1)
                if not plan.first:
                    store(plan, "prev_out2", i - 1)
                    store(plan, "prev_out3", i - 1)
                load_residual(i, 0)
                for name in plan.names:
                    if name.startswith("next_qk"):
                        restack(plan, name)
                    elif name.startswith("out"):
                        store(plan, name, i)
                load_residual(i, 1)

            image1(0)
            with sp.Fori(1, IMAGES - 1) as i:
                image1(i)
            image1(IMAGES - 1)
            for side, name in enumerate(EPILOGUE_OUT):
                cols = slice(side * SIDE, (side + 1) * SIDE)
                evacuated(plan_epilogue, name)
                sp.dma_start(out[IMAGES - 1, :, :, H:2 * H][:, :, cols].rearrange("k p n -> p k n"),
                             y_res[:, :, cols]).then_inc(out_stored, 16)
            sp.wait_ge(out_stored, FREE_CREDIT + IMAGES * 64)

        @block.gpsimd
        def _(pool):
            pool.sem_inc(o_split, FREE_CREDIT)
            nc.gpsimd.memset(ident[:, :], 0.0).then_inc(consts_ready, 1)
            nc.gpsimd.memset(gavg[:, :], 1.0 / GROUP).then_inc(consts_ready, 1)
            pool.wait_ge(consts_ready, 2)
            nc.gpsimd.affine_select(out=ident[:, :], in_=ident[:, :], compare_op=ALU.not_equal, fill=1.0,
                                    base=0, pattern=[[-1, P]], channel_multiplier=1).then_inc(consts_ready, 1)
            groups = gavg[:, :].rearrange("p (g c) -> p g c", c=GROUP)
            nc.gpsimd.affine_select(out=groups, in_=groups, compare_op=ALU.is_ge, fill=0.0, base=0,
                                    pattern=[[-GROUP, P // GROUP], [0, GROUP]], channel_multiplier=1).then_inc(consts_ready, 1)
            nc.gpsimd.memset(minus_half[:, :, :], -0.5).then_inc(consts_ready, 1)
            pool.wait_ge(consts_ready, 5)
            nc.gpsimd.affine_select(out=groups, in_=groups, compare_op=ALU.is_ge, fill=0.0, base=GROUP - 1,
                                    pattern=[[GROUP, P // GROUP], [0, GROUP]], channel_multiplier=-1).then_inc(consts_ready, 1)

            def wait_scalar(semaphore, value):
                pool.wait_ge(semaphore, value)
                pool.sem_inc(pool_steps, 1)

            def normalise(t0, t):
                wait_scalar(rsum_ready, t0 + t + 1)
                p = prob[:, t % 2, :]
                nc.gpsimd.tensor_scalar(p, p, rsum[:, t % 2:t % 2 + 1], 1.0, ALU.mult, ALU.mult)\
                    .then_inc(prob_ready, 1)

            def norm_chunk(n, c):
                k, half = c // 2, c % 2
                if c == 0:
                    wait_scalar(y_loaded, 16 * n + 16)
                    wait_scalar(gn_affine, n + 1)
                y = y_in[:, k, half, :]
                nc.gpsimd.tensor_scalar(y, y, gn_now[:, k:k + 1], gn_now[:, KT + k:KT + k + 1],
                                        ALU.mult, ALU.add).then_inc(h_full, 1)

            def norm_chunk_low(n, c):
                pool.wait_ge(h_high, 4 * n + c + 1)
                h_difference(nc.gpsimd, c)

            def norm_root(n):
                images = slice(*GN_SETS[n])
                pool.wait_ge(gn_var_ready, n + 1)
                nc.gpsimd.tensor_tensor(gn_root[:, images, :], gn_var[:, images, :], minus_half[:, images, :],
                                        ALU.pow).then_inc(gn_root_ready, 1)

            def norm_step(n, s):
                if s - 2 in NORM_STEPS1:
                    norm_chunk_low(n, NORM_STEPS1.index(s - 2))
                if s in NORM_STEPS1:
                    norm_chunk(n, NORM_STEPS1.index(s))

            with pool.Fori(0, IMAGES - 1) as i:
                for t in range(T0_IMAGE):
                    normalise(T0_IMAGE * i, t)
            for t in range(T0_IMAGE):
                if t == 2:
                    norm_root(0)
                normalise(T0_IMAGE * (IMAGES - 1), t)
                if t in NORM_STEPS0:
                    norm_chunk(0, NORM_STEPS0.index(t))
            normalise(T1_BASE, 0)

            def pair_low(i, j):
                pool.wait_ge(o_high, 4 * i + j // 2 + 1)
                pair_difference(nc.gpsimd, (j // 2) % 2)

            def pairs_of(i, names):
                for name in names:
                    if name in PAIR_ENDS:
                        pair_low(i - 1 if name == "prev_av7" else i, int(name[-1]))

            def image1(i):
                plan = plan1(i)
                for s in range(T1_IMAGE):
                    if s + 1 < T1_IMAGE - DVE_TILES or not plan.last:
                        normalise(T1_BASE + T1_IMAGE * i, s + 1)
                    if plan.first and s == NORM_ROOT_STEP:
                        norm_root(1)
                    if not plan.last:
                        norm_step(i + 1, s)
                    if s >= PAIR_BEHIND:
                        pairs_of(i, [name for name in head_outputs(STEPS1[s - PAIR_BEHIND]) if plan.has(name)])

            image1(0)
            with pool.Fori(1, IMAGES - 1) as i:
                image1(i)
            image1(IMAGES - 1)

        @block.scalar
        def _(act):
            act.sem_inc(exp_ready, EXP_CREDIT)

            def wait_acc(number):
                act.wait_ge(acc_done, GROUP_CREDIT + number + 1)

            def exp(t0, t):
                act.wait_ge(max_ready, t0 + t + 1)
                act.wait_ge(transposed, TRANS_CREDIT + 2 * (t0 + t) - 2)
                nc.scalar.activation(prob[:, t % 2, :], scores[:, t % 2, :], ACT.Exp,
                                     bias=negmax[:, t % 2:t % 2 + 1], scale=1.0,
                                     accum_out=rowsum[:, t % 2:t % 2 + 1]).then_inc(exp_ready, 1)

            def trans_high(t0, t, av_before):
                if t % 4 == 0 and av_before is not None:
                    wait_acc(av_before)
                for h in range(2):
                    act.wait_ge(transposed, TRANS_CREDIT + 2 * (t0 + t) + h + 1)
                    nc.scalar.activation(pt_block(pt_hi, (t // 4) % 2, t, h),
                                         trans[:, h, :].rearrange("p (j n) -> p j n", n=P),
                                         ACT.Copy).then_inc(pt_high, 1)

            def weight_high(w):
                nc.scalar.activation(flat(w_hi[w]), flat(w_raw[w]), ACT.Copy,
                                     scale=QSCALE if w == "q" else 1.0).then_inc(w_high, 1)

            def x_part_high(i, half):
                act.wait_ge(x_loaded[half], 16 * i + 16)
                cols = slice(half * H, (half + 1) * H)
                nc.scalar.activation(x_hi[:, :, cols], x_raw[:, :, cols], ACT.Copy).then_inc(x_high, 1)

            def high(dst, plan, name):
                wait_acc(plan.number(name))
                nc.scalar.activation(dst, acc[:, plan.bank(name), :], ACT.Copy).then_inc(acc_high, 1)

            def a_high(plan, name):
                a = int(name[-1])
                high(a_hi[:, a % 2, (a // 2) * H:(a // 2 + 1) * H], plan, name)

            act.wait_ge(w_loaded, 2 * 16)
            weight_high("b")
            weight_high("c")
            x_part_high(0, 0)
            for ct in range(KT):
                wait_acc(ct)
                nc.scalar.activation(wk_hi[:, ct, :], acc[:, ct, 0:C], ACT.Copy).then_inc(acc_high, 1)
            x_part_high(0, 1)
            act.wait_ge(later_loaded, 16)
            for name, w in zip(FIRST_A, LATER_WEIGHTS):
                a_high(plan_first_a, name)
                weight_high(w)
            weight_high(LATER_WEIGHTS[-1])

            def chunk_high(plan, name, i):
                r = int(name[-1])
                act.wait_ge(qk_stacked[r % 2], FREE_CREDIT + QK_IMAGE * i + CHUNK_DMA * (r // 2))
                wait_acc(plan.number(name))
                nc.scalar.activation(qk[:, r % 2, 0, :], acc[:, plan.bank(name), :], ACT.Identity,
                                     bias=qk_bias(r), scale=1.0).then_inc(acc_high, 1)

            def norm_chunk_high(n, c):
                k, half = c // 2, c % 2
                act.wait_ge(h_full, 4 * n + c + 1)
                nc.scalar.activation(h_hi[:, k, half * H:(half + 1) * H], y_in[:, k, half, :], ACT.Copy)\
                    .then_inc(h_high, 1)

            def image0(i, last):
                plan, t0 = plan0(i, last), T0_IMAGE * i

                def trans(t):
                    before = BASES["layer0"] + len(LAYER0) * (i - 1) + LAYER0.index("av3" if t >= 4 else "av1")
                    trans_high(t0, t, before)

                for s in range(T0_IMAGE):
                    if s >= LAG:
                        trans(s - LAG)
                    exp(t0, s)
                    if last and s - 1 in NORM_STEPS0:
                        norm_chunk_high(0, NORM_STEPS0.index(s - 1))
                    if s in D_STEPS:
                        n = D_STEPS.index(s)
                        high(d_part(d_hi, n), plan, f"d{n}")
                for name in ends(TAIL0_LAST if last else TAIL0):
                    n = int(name[-1])
                    if name == "s1":
                        exp(T1_BASE, 0)
                    elif name.startswith("t"):
                        trans(n)
                        if name == "t7" and not last:
                            for half in range(X_HALVES):
                                x_part_high(i + 1, half)
                    elif name.startswith("next_a"):
                        a_high(plan, name)
                    elif name.startswith("next_qk"):
                        chunk_high(plan, name, 0)

            with act.Fori(0, IMAGES - 1) as i:
                image0(i, False)
            image0(IMAGES - 1, True)

            def values_high(plan, name):
                v = int(name[-1])
                wait_acc(plan.number(name))
                for j in range(2):
                    ins = nc.scalar.activation(
                        v_st[:, 2 * v + j, :, 0, :],
                        acc[:, plan.bank(name), j * C:(j + 1) * C].rearrange("p (h d) -> p h d", d=HD), ACT.Copy)
                ins.then_inc(acc_high, 1)

            def output_rows(plan, name, i):
                j = int(name[-1])
                pair = (j // 2) % 2
                rows = slice((j % 2) * HD, (j % 2 + 1) * HD)
                wait_acc(plan.number(name))
                if j % 2 == 0:
                    act.wait_ge(o_split, FREE_CREDIT + 4 * i + max(j // 2 - 1, 0))
                nc.scalar.activation(o_sum[rows, pair, :], acc[HD:2 * HD, plan.bank(name), :], ACT.Identity,
                                     bias=vec[rows, BV + pair:BV + pair + 1], scale=1.0).then_inc(o_part, 1)

            def pair_high(plan, name, i):
                pair = (int(name[-1]) // 2) % 2
                act.wait_ge(acc_evac, EVAC_CREDIT + plan.number(name) + 1)
                nc.scalar.activation(o_hi[:, pair, :], o_sum[:, pair, :], ACT.Copy).then_inc(o_high, 1)

            def pairs_of(plan, step, i):
                for name in ends(step):
                    if plan.has(name) and name in PAIR_ENDS:
                        pair_high(plan, name, i - 1 if name == "prev_av7" else i)

            def evacuate(plan, names, i):
                for name in names:
                    if not plan.has(name):
                        continue
                    if name.startswith("next_qk"):
                        chunk_high(plan, name, i + 1)
                    elif name.startswith(("qk", "first_qk")):
                        chunk_high(plan, name, i)
                    elif name.startswith("v"):
                        values_high(plan, name)
                    elif name == "prev_av7":
                        output_rows(plan, name, i - 1)
                    elif name.startswith("av"):
                        output_rows(plan, name, i)

            exp(T1_BASE, 1)

            def image1(i):
                plan, t1 = plan1(i), T1_BASE + T1_IMAGE * i
                for s in range(T1_IMAGE):
                    j = s // 4
                    if j >= 2:
                        before = plan.number(f"av{j - 2}")
                    elif plan.first:
                        before = None
                    elif j == 1:
                        before = plan.number("prev_av7")
                    else:
                        before = plan.base - (LAYER1[::-1].index("av6") + 1)
                    if s >= SUM_BEHIND:
                        evacuate(plan, head_outputs(STEPS1[s - SUM_BEHIND]), i)
                    if s >= PAIR_BEHIND:
                        pairs_of(plan, STEPS1[s - PAIR_BEHIND], i)
                    if plan.last and s == T1_IMAGE - 1:
                        evacuate(plan, head_outputs(STEPS1[s]), i)
                    trans_high(t1, s, before)
                    if s + LAG < T1_IMAGE or not plan.last:
                        exp(t1, s + LAG)
                    if not plan.last and s - 1 in NORM_STEPS1:
                        norm_chunk_high(i + 1, NORM_STEPS1.index(s - 1))
                    evacuate(plan, other_groups(STEPS1[s]), i)
                if not plan.last:
                    evacuate(plan, head_outputs(STEPS1[T1_IMAGE - 1]), i)

            image1(0)
            with act.Fori(1, IMAGES - 1) as i:
                image1(i)
            image1(IMAGES - 1)
            for side, name in enumerate(EPILOGUE_AV):
                cols = slice(side * SIDE, (side + 1) * SIDE)
                wait_acc(plan_epilogue.number(name))
                nc.scalar.activation(o_sum[HD:2 * HD, 1, cols], acc[HD:2 * HD, plan_epilogue.bank(name), 0:SIDE],
                                     ACT.Identity, bias=vec[HD:2 * HD, BV + 1:BV + 2], scale=1.0).then_inc(o_part, 1)
                act.wait_ge(acc_evac, EVAC_CREDIT + plan_epilogue.number(name) + 1)
                nc.scalar.activation(o_hi[:, 1, cols], o_sum[:, 1, cols], ACT.Copy).then_inc(o_high, 1)

        @block.vector
        def _(dve):
            dve.sem_inc(acc_evac, EVAC_CREDIT)
            dve.sem_inc(pt_split, SPLIT_CREDIT)

            def row_max(t0, t):
                dve.wait_ge(scores_ready, t0 + t + 1)
                nc.vector.tensor_reduce(negmax[:, t % 2:t % 2 + 1], scores[:, t % 2, :], AX_X, ALU.max,
                                        negate=True).then_inc(max_ready, 1)

            def recip(t0, t):
                dve.wait_ge(exp_ready, EXP_CREDIT + t0 + t + 1)
                nc.vector.reciprocal(rsum[:, t % 2:t % 2 + 1], rowsum[:, t % 2:t % 2 + 1]).then_inc(rsum_ready, 1)

            def normalise_last(t0, t):
                dve.wait_ge(rsum_ready, t0 + t + 1)
                p = prob[:, t % 2, :]
                nc.vector.tensor_scalar(p, p, rsum[:, t % 2:t % 2 + 1], 1.0, ALU.mult, ALU.mult)\
                    .then_inc(last_prob_ready, 1)

            def trans_low(t0, t):
                for h in range(2):
                    dve.wait_ge(pt_high, 2 * (t0 + t) + h + 1)
                    slot = (t // 4) % 2
                    nc.vector.tensor_tensor(pt_block(pt_lo, slot, t, h),
                                            trans[:, h, :].rearrange("p (j n) -> p j n", n=P),
                                            pt_block(pt_hi, slot, t, h).bitcast(F32),
                                            ALU.subtract).then_inc(pt_split, 1)

            def wait_acc(number):
                dve.wait_ge(acc_done, GROUP_CREDIT + number + 1)

            links = [0]

            def link(instructions):
                for ins in instructions:
                    ins.then_inc(gn_chain, 1)
                links[0] += len(instructions)
                dve.wait_ge(gn_chain, links[0])

            def norm_channels(n):
                first, end = GN_SETS[n]
                for m in range(KT * first, KT * end):
                    nc.vector.bn_aggr(gn_mv[:, m // KT, m % KT, :], y_stats[:, m * 12:(m + 1) * 12])\
                        .then_inc(gn_stats, 1)

            def norm_deviations(n, plan, name="gn0"):
                images = slice(*GN_SETS[n])
                size = GN_SETS[n][1] - GN_SETS[n][0]
                avg = acc[:, plan.bank(name), 0:size * KT * 2].rearrange("p (i k v) -> p i k v", k=KT, v=2)
                wait_acc(plan.number(name))
                nc.vector.tensor_copy(gn_mean[:, images, :], avg[:, :, :, 0]).then_inc(gn_chain, 1)
                links[0] += 1
                nc.vector.tensor_copy(gn_var[:, images, :], avg[:, :, :, 1]).then_inc(acc_evac, 1)
                dve.wait_ge(gn_chain, links[0])
                link([nc.vector.tensor_tensor(gn_dev[:, images, :], gn_mv[:, images, :, 0], gn_mean[:, images, :],
                                              ALU.subtract)])
                nc.vector.tensor_tensor(gn_sqdev[:, images, :], gn_dev[:, images, :], gn_dev[:, images, :],
                                        ALU.mult).then_inc(gn_dev_ready, 1)

            def norm_variance(n, plan, name="gn1"):
                images = slice(*GN_SETS[n])
                size = GN_SETS[n][1] - GN_SETS[n][0]
                dev = acc[:, plan.bank(name), 0:size * KT].rearrange("p (i k) -> p i k", k=KT)
                wait_acc(plan.number(name))
                dve.wait_ge(acc_evac, EVAC_CREDIT + plan.number(name.replace("1", "0")) + 1)
                nc.vector.scalar_tensor_tensor(gn_var[:, images, :], dev, EPS, gn_var[:, images, :],
                                               ALU.add, ALU.add).then_inc(acc_evac, 1)
                dve.wait_ge(acc_evac, EVAC_CREDIT + plan.number(name) + 1)
                dve.sem_inc(gn_var_ready, 1)

            def norm_affine(n):
                first, end = GN_SETS[n]
                dve.wait_ge(gn_root_ready, n + 1)
                images = range(first, end)
                link([nc.vector.tensor_tensor(gn_scale[:, m, 0:KT], gn_root[:, m, :], vec[:, GNW:GNW + KT],
                                              ALU.mult) for m in images])
                link([nc.vector.tensor_tensor(gn_scale[:, m, KT:2 * KT], gn_mean[:, m, :],
                                              gn_scale[:, m, 0:KT], ALU.mult) for m in images])
                link([nc.vector.tensor_tensor(gn_scale[:, m, KT:2 * KT], vec[:, GNB:GNB + KT],
                                              gn_scale[:, m, KT:2 * KT], ALU.subtract) for m in images])

            def norm_low(c):
                dve.wait_ge(h_high, c + 1)
                h_difference(nc.vector, c)

            def norm_next(m):
                nc.vector.tensor_copy(gn_now[:, :], gn_scale[:, m, :]).then_inc(gn_affine, 1)

            def weight_low(w):
                dve.wait_ge(w_high, WEIGHTS.index(w) + 1)
                nc.vector.scalar_tensor_tensor(flat(w_lo[w]), flat(w_raw[w]), QSCALE if w == "q" else 1.0,
                                               flat(w_hi[w]).bitcast(F32), ALU.mult, ALU.subtract).then_inc(w_split, 1)

            def x_part_low(i, half):
                dve.wait_ge(x_high, X_HALVES * i + half + 1)
                cols = slice(half * H, (half + 1) * H)
                nc.vector.tensor_tensor(x_lo[:, :, cols], x_raw[:, :, cols], x_hi[:, :, cols].bitcast(F32),
                                        ALU.subtract).then_inc(x_split, 1)

            def low(lo, hi, plan, name, highs):
                dve.wait_ge(acc_high, highs)
                nc.vector.tensor_tensor(lo, acc[:, plan.bank(name), :], hi.bitcast(F32),
                                        ALU.subtract).then_inc(acc_evac, 1)

            def a_low(plan, name, highs):
                a = int(name[-1])
                cols = slice((a // 2) * H, (a // 2 + 1) * H)
                low(a_lo[:, a % 2, cols], a_hi[:, a % 2, cols], plan, name, highs)

            weight_low("b")
            weight_low("c")
            x_part_low(0, 0)
            for ct in range(KT):
                dve.wait_ge(acc_high, ct + 1)
                nc.vector.tensor_tensor(wk_lo[:, ct, :], acc[:, ct, 0:C], wk_hi[:, ct, :].bitcast(F32),
                                        ALU.subtract).then_inc(acc_evac, 1)
            x_part_low(0, 1)
            for n, (name, w) in enumerate(zip(FIRST_A, LATER_WEIGHTS)):
                a_low(plan_first_a, name, KT + n + 1)
                weight_low(w)
            weight_low(LATER_WEIGHTS[-1])
            dve.wait_ge(vec_loaded, 16)
            nc.vector.tensor_scalar(bq8[:, :], vec[:, BQ:BQ + 2], QSCALE, None, ALU.mult).then_inc(w_split, 1)

            HIGH0 = KT + len(FIRST_A)
            KINDS0, KINDS1 = ("d", "a0", "a1", "a2", "a3", "qk"), ("v", "qk")
            HIGH_IMAGE0 = plan0(0).until(LAYER0[-1], KINDS0)
            HIGH_LAYER0 = HIGH0 + HIGH_IMAGE0 * (IMAGES - 1) + plan0(IMAGES - 1, True).until("next_qk5", KINDS0)
            HIGH_IMAGE1 = plan1(1).until(plan1(1).names[-1], KINDS1)

            def chunk_low(plan, name, highs):
                r = int(name[-1])
                dve.wait_ge(acc_high, highs)
                nc.vector.scalar_tensor_tensor(qk[:, r % 2, 1, :], acc[:, plan.bank(name), :], qk_bias(r),
                                               qk[:, r % 2, 0, :].bitcast(F32),
                                               ALU.add, ALU.subtract).then_inc(acc_evac, 1)

            def image0(i, last):
                plan, t0 = plan0(i, last), T0_IMAGE * i

                highs = HIGH0 + HIGH_IMAGE0 * i

                def result(a):
                    if a == 0:
                        dve.wait_ge(res_loaded, 64 * i + 64)
                    wait_acc(plan.number(f"av{a}"))
                    nc.vector.scalar_tensor_tensor(y_out[:, a, :], acc[:, plan.bank(f"av{a}"), :],
                                                   vec[:, GAMMA:GAMMA + 1], y_out[:, a, :],
                                                   ALU.mult, ALU.add).then_inc(acc_evac, 1)
                    dve.wait_ge(acc_evac, EVAC_CREDIT + plan.number(f"av{a}") + 1)
                    col = ((i * KT + a % 2) * 2 + a // 2) * 6
                    nc.vector.bn_stats(y_stats[:, bass.ds(col, 6)], y_out[:, a, :]).then_inc(y_ready, 1)

                if last:
                    dve.wait_ge(y_ready, 4 * (IMAGES - 1))
                    norm_channels(0)
                for s in range(T0_IMAGE):
                    if s >= 1:
                        recip(t0, s - 1)
                    row_max(t0, s)
                    if s - 1 in D_STEPS:
                        n = D_STEPS.index(s - 1)
                        low(d_part(d_lo, n), d_part(d_hi, n), plan, f"d{n}", highs + plan.until(f"d{n}", KINDS0))
                    if last and s - 2 in NORM_STEPS0:
                        norm_low(NORM_STEPS0.index(s - 2))
                    if s >= LAG:
                        trans_low(t0, s - LAG)
                    if last and s == 0:
                        norm_deviations(0, plan)
                    if last and s == 1:
                        norm_variance(0, plan)
                    if last and s == 2:
                        norm_affine(0)
                        norm_next(0)
                recip(t0, T0_IMAGE - 1)
                if last:
                    norm_low(3)
                for name in ends(TAIL0_LAST if last else TAIL0):
                    n = int(name[-1])
                    if name.startswith("s"):
                        if n == 1:
                            recip(T1_BASE, 0)
                        row_max(T1_BASE, n)
                    elif name.startswith("t"):
                        trans_low(t0, n)
                        if name == "t7" and not last:
                            for half in range(X_HALVES):
                                x_part_low(i + 1, half)
                    elif name.startswith("av"):
                        result(n)
                    elif name.startswith("next_a"):
                        a_low(plan, name, highs + plan.until(name, KINDS0))
                    else:
                        chunk_low(plan, name, highs + plan.until(name, KINDS0))

            with dve.Fori(0, IMAGES - 1) as i:
                image0(i, False)
            image0(IMAGES - 1, True)
            dve.wait_ge(y_ready, 4 * IMAGES)
            norm_channels(1)

            def values_low(plan, name, highs):
                v = int(name[-1])
                dve.wait_ge(acc_high, highs)
                for j in range(2):
                    ins = nc.vector.tensor_tensor(
                        v_st[:, 2 * v + j, :, 1, :],
                        acc[:, plan.bank(name), j * C:(j + 1) * C].rearrange("p (h d) -> p h d", d=HD),
                        v_st[:, 2 * v + j, :, 0, :].bitcast(F32), ALU.subtract)
                ins.then_inc(acc_evac, 1)

            def output_add(plan, name, i):
                j = int(name[-1])
                pair = (j // 2) % 2
                rows = slice((j % 2) * HD, (j % 2 + 1) * HD)
                dve.wait_ge(o_part, 8 * i + j + 1)
                nc.vector.tensor_tensor(o_sum[rows, pair, :], acc[0:HD, plan.bank(name), :],
                                        o_sum[rows, pair, :], ALU.add).then_inc(acc_evac, 1)

            def result(plan, name, i):
                n = int(name[-1])
                o = n % 2
                wait_acc(plan.number(name))
                dve.wait_ge(yres_loaded, 64 * i + 32 * (n // 2) + 32)
                nc.vector.scalar_tensor_tensor(y_res[:, o, :], acc[:, plan.bank(name), :],
                                               vec[:, BP + o:BP + o + 1], y_res[:, o, :],
                                               ALU.add, ALU.add).then_inc(acc_evac, 1)

            def evacuate(plan, names, i, highs_before):
                for name in names:
                    if not plan.has(name):
                        continue
                    highs = highs_before + plan.until(name, KINDS1)
                    if name == "first_gn0":
                        norm_deviations(1, plan, name)
                    elif name == "first_gn1":
                        norm_variance(1, plan, name)
                    elif "qk" in name:
                        chunk_low(plan, name, highs)
                    elif name.startswith("v"):
                        values_low(plan, name, highs)
                    elif name == "prev_av7":
                        output_add(plan, name, i - 1)
                    elif name.startswith("av"):
                        output_add(plan, name, i)
                    elif name.startswith("prev_out"):
                        result(plan, name, i - 1)
                    else:
                        result(plan, name, i)


            def image1(i):
                plan, t1 = plan1(i), T1_BASE + T1_IMAGE * i
                highs = HIGH_LAYER0 + (0 if plan.first else 1 + HIGH_IMAGE1 * i)
                for s in range(T1_IMAGE):
                    if s + 1 < T1_IMAGE or not plan.last:
                        recip(t1, s + 1)
                        if plan.last and s + 1 >= T1_IMAGE - DVE_TILES:
                            normalise_last(t1, s + 1)
                    late = plan.first and s < AV_PARTS
                    if s >= SUM_BEHIND and not late:
                        evacuate(plan, other_groups(STEPS1[s - SUM_BEHIND]), i, highs)
                    if s + LAG < T1_IMAGE or not plan.last:
                        row_max(t1, s + LAG)
                    if s >= SUM_BEHIND and late:
                        evacuate(plan, other_groups(STEPS1[s - SUM_BEHIND]), i, highs)
                    if plan.last and s == T1_IMAGE - 1:
                        evacuate(plan, head_outputs(STEPS1[s]), i, highs)
                    trans_low(t1, s)
                    if s >= SUM_BEHIND:
                        evacuate(plan, head_outputs(STEPS1[s - SUM_BEHIND]), i, highs)
                    if s == 1 and not plan.last:
                        dve.wait_ge(h_split, 4 * i + 4)
                        norm_next(i + 1)
                    if s == NORM_AFFINE_STEP and plan.first:
                        norm_affine(1)
                if not plan.last:
                    evacuate(plan, ends(STEPS1[T1_IMAGE - 1]), i, highs)

            image1(0)
            with dve.Fori(1, IMAGES - 1) as i:
                image1(i)
            image1(IMAGES - 1)
            for side, name in enumerate(EPILOGUE_AV):
                cols = slice(side * SIDE, (side + 1) * SIDE)
                dve.wait_ge(o_part, 8 * IMAGES + side)
                nc.vector.tensor_tensor(o_sum[HD:2 * HD, 1, cols], acc[0:HD, plan_epilogue.bank(name), 0:SIDE],
                                        o_sum[HD:2 * HD, 1, cols], ALU.add).then_inc(acc_evac, 1)
                dve.wait_ge(o_high, 4 * IMAGES + side)
                nc.vector.tensor_tensor(o_lo[:, 1, cols], o_sum[:, 1, cols], o_hi[:, 1, cols].bitcast(F32),
                                        ALU.subtract).then_inc(side_split, 1)
            dve.wait_ge(yres_loaded, 64 * IMAGES)
            for side, name in enumerate(EPILOGUE_OUT):
                cols = slice(side * SIDE, (side + 1) * SIDE)
                wait_acc(plan_epilogue.number(name))
                for o in range(KT):
                    ins = nc.vector.scalar_tensor_tensor(
                        y_res[:, o, cols], acc[:, plan_epilogue.bank(name), o * SIDE:(o + 1) * SIDE],
                        vec[:, BP + o:BP + o + 1], y_res[:, o, cols], ALU.add, ALU.add)
                ins.then_inc(acc_evac, 1)

        @block.tensor
        def _(pe):
            pe.sem_inc(transposed, TRANS_CREDIT)
            pe.sem_inc(acc_done, GROUP_CREDIT)

            def run(dst, pairs, starts=True, stops=True):
                for n, (w, m) in enumerate(pairs):
                    ins = nc.tensor.matmul(dst, w, m, start=(starts and n == 0),
                                           stop=(stops and n == len(pairs) - 1))
                return ins

            def bank_free(plan, name):
                pe.wait_ge(acc_evac, EVAC_CREDIT + plan.before(name) + 1)

            def group(plan, name, pairs, cols=slice(0, H), part=0, parts=1):
                if part == 0:
                    bank_free(plan, name)
                size = len(pairs) // parts
                ins = run(acc[:, plan.bank(name), cols], pairs[part * size:(part + 1) * size],
                          part == 0, part == parts - 1)
                if part == parts - 1:
                    ins.then_inc(acc_done, 1)

            def evacuated(number):
                pe.wait_ge(acc_evac, EVAC_CREDIT + number + 1)

            def over_k(w, m):
                return [pair for k in range(KT)
                        for pair in products((w(0, k), m(0, k)), (w(1, k), m(1, k)))]

            def transpose_tile(t0, t, last=False):
                if last and t >= T1_IMAGE - DVE_TILES:
                    pe.wait_ge(last_prob_ready, t - (T1_IMAGE - DVE_TILES) + 1)
                else:
                    pe.wait_ge(prob_ready, t0 + t + 1)
                for h in range(2):
                    pe.wait_ge(pt_split, 2 * (t0 + t) + h + 1)
                    for b in range(4):
                        j = 4 * h + b
                        ins = nc.tensor.transpose(trans[:, h, b * P:(b + 1) * P],
                                                  prob[:, t % 2, j * P:(j + 1) * P], ident[:, :])
                    ins.then_inc(transposed, 1)

            w = lambda name: (lambda part, k, cols: (w_hi, w_lo)[part][name][:, k, cols])
            wb, wc, wd, wq, wk, wv, wp = (w(n) for n in "bcdqkvp")
            abc = lambda part, k, cols: (wk_hi, wk_lo)[part][:, k, cols]
            col = lambda n, size: slice(n * size, (n + 1) * size)

            pe.wait_ge(w_split, 2)
            for ct in range(KT):
                run(acc[:, ct, 0:C], over_k(lambda part, k: wb(part, k, col(ct, P)),
                                            lambda part, k: wc(part, k, slice(0, C)))).then_inc(acc_done, 1)
            pe.wait_ge(consts_ready, 6)
            evacuated(1)

            def a_group(plan, name):
                a = int(name[-1])
                group(plan, name, over_k(lambda part, k: abc(part, k, col(a % 2, P)),
                                         lambda part, k: (x_hi, x_lo)[part][:, k, col(a // 2, H)]))

            for n, name in enumerate(FIRST_A):
                if n % 2 == 0:
                    pe.wait_ge(x_split, n // 2 + 1)
                a_group(plan_first_a, name)

            h_part = lambda part, k, cols: (h_hi, h_lo)[part][:, k, cols]

            def chunk(plan, name, part=0, parts=1):
                r = int(name[-1])
                wt = wk if r % 4 >= 2 else wq
                group(plan, name, over_k(lambda part, k: wt(part, k, col(r // 4, P)),
                                         lambda part, k: h_part(part, k, col(r % 2, H))),
                      part=part, parts=parts)

            def norm_group(plan, name, n, src, width):
                first, end = GN_SETS[n]
                rhs = src[:, first:end].rearrange("p i k v -> p (i k v)" if width == 2 else "p i k -> p (i k)")
                group(plan, name, [(gavg[:, :], rhs)], slice(0, (end - first) * KT * width))

            def two_tiles(plan, name, n, source, weight):
                bank_free(plan, name)
                for j in range(2):
                    ins = run(acc[:, plan.bank(name), col(j, C)],
                              over_k(lambda part, k: source(part, k, col(2 * n + j, P)),
                                     lambda part, k: weight(part, k, slice(0, C))))
                ins.then_inc(acc_done, 1)

            def scores1(i, t1, s):
                head, tile = (s // 4) % 4, 4 * (s // 16) + s % 4
                if s in (0, 8):
                    for slot in range(2):
                        pe.wait_ge(qk_stacked[slot], FREE_CREDIT + QK_IMAGE * i + CHUNK_DMA * (2 if s == 0 else 4))
                pe.wait_ge(exp_ready, t1 + s + 1)
                for mh in range(2):
                    ins = run(scores[:, s % 2, col(mh, H)],
                              [(q_st[:, head, col(tile, P)], k_st[:, part, head, col(mh, H)]) for part in range(2)])
                ins.then_inc(scores_ready, 1)

            def image0(i, last):
                plan, t0 = plan0(i, last), T0_IMAGE * i

                def scores0(s):
                    pe.wait_ge(exp_ready, t0 + s + 1)
                    for mh in range(2):
                        ins = run(scores[:, s % 2, col(mh, H)],
                                  over_k(lambda part, k: (a_hi, a_lo)[part][:, k, col(s, P)],
                                         lambda part, k: (x_hi, x_lo)[part][:, k, col(mh, H)]))
                    ins.then_inc(scores_ready, 1)

                def values(n, part, parts):
                    half, ct = n // 2, n % 2
                    if ct == 0 and part == 0:
                        pe.wait_ge(pt_split, SPLIT_CREDIT + 2 * t0 + 8 * (half + 1))
                    group(plan, f"av{n}", [
                        pair for j in range(NT)
                        for pair in products((d_hi[:, j, col(ct, P)], pt_hi[:, half, j, :]),
                                             (d_lo[:, j, col(ct, P)], pt_lo[:, half, j, :]))],
                        part=part, parts=parts)

                def project_d(n):
                    if n == 0:
                        pe.wait_ge(w_split, len(WEIGHTS) + 1)
                    two_tiles(plan, f"d{n}", n, lambda part, k, cols: (x_hi, x_lo)[part][:, k, cols], wd)

                for s in range(T0_IMAGE):
                    if s == 0:
                        evacuated(plan.base - 3)
                    if s == 4:
                        evacuated(plan.base - 1)
                    scores0(s)
                    if last and s == 0:
                        pe.wait_ge(gn_stats, KT * GN_SETS[0][1])
                        norm_group(plan, "gn0", 0, gn_mv, 2)
                    if last and s == 1:
                        pe.wait_ge(gn_dev_ready, 1)
                        norm_group(plan, "gn1", 0, gn_sqdev, 1)
                    if s >= LAG:
                        transpose_tile(t0, s - LAG)
                    if s in D_STEPS:
                        project_d(D_STEPS.index(s))
                evacuated(plan.number("d3"))
                for g in TAIL0_LAST if last else TAIL0:
                    name, part, parts = g if not isinstance(g, str) else (g, 0, 1)
                    n = int(name[-1])
                    if name.startswith("s"):
                        scores1(0, T1_BASE, n)
                    elif name.startswith("t"):
                        transpose_tile(t0, n)
                    elif name.startswith("av"):
                        values(n, part, parts)
                    elif name.startswith("next_a"):
                        if n == 0:
                            pe.wait_ge(x_split, X_HALVES * (i + 2))
                        a_group(plan, name)
                    else:
                        if n == 0:
                            pe.wait_ge(h_split, 4)
                        chunk(plan, name)

            with pe.Fori(0, IMAGES - 1) as i:
                image0(i, False)
            image0(IMAGES - 1, True)

            def project_v(plan, name):
                two_tiles(plan, name, int(name[-1]), h_part, wv)

            def values(plan, name, part, parts, t1):
                j = int(name[-1])
                if part == 0:
                    pe.wait_ge(pt_split, SPLIT_CREDIT + 2 * t1 + 8 * (j + 1))
                if name == "av0":
                    evacuated(plan.number(f"v{part}"))
                group(plan, name, [(v_st[:, b, j % 4, :, :].rearrange("p v d -> p (v d)"), src[:, j % 2, b, :])
                                   for b in range(NT) for src in (pt_hi, pt_lo)], part=part, parts=parts)

            def project_out(plan, name, i, part, parts):
                n = int(name[-1])
                if n % 2 == 0:
                    pe.wait_ge(o_split, FREE_CREDIT + 4 * i + n + 2)
                group(plan, name, over_k(lambda part, k: wp(part, k, col(n % 2, P)),
                                         lambda part, k: (o_hi, o_lo)[part][:, k, :]), part=part, parts=parts)

            def run_groups(plan, step, i, t1):
                for g in step:
                    name, part, parts = g if not isinstance(g, str) else (g, 0, 1)
                    if not plan.has(name):
                        continue
                    if name == "next_qk0":
                        pe.wait_ge(h_split, 4 * i + 8)
                    if name == "first_gn0":
                        pe.wait_ge(gn_stats, KT * IMAGES)
                        norm_group(plan, name, 1, gn_mv, 2)
                    elif name == "first_gn1":
                        pe.wait_ge(gn_dev_ready, 2)
                        norm_group(plan, name, 1, gn_sqdev, 1)
                    elif "qk" in name:
                        chunk(plan, name, part, parts)
                    elif name == "prev_av7":
                        values(plan, name, part, parts, t1 - T1_IMAGE)
                    elif name.startswith("av"):
                        values(plan, name, part, parts, t1)
                    elif name.startswith("v"):
                        project_v(plan, name)
                    elif name.startswith("prev_out"):
                        project_out(plan, name, i - 1, part, parts)
                    else:
                        project_out(plan, name, i, part, parts)


            def image1(i):
                plan, t1 = plan1(i), T1_BASE + T1_IMAGE * i
                for s in range(T1_IMAGE):
                    if plan.first and s == 0:
                        run_groups(plan, STEPS1[s], i, t1)
                    if s + LAG < T1_IMAGE:
                        scores1(i, t1, s + LAG)
                    elif not plan.last:
                        scores1(i + 1, t1 + T1_IMAGE, s + LAG - T1_IMAGE)
                    if plan.last and s == T1_IMAGE - 1:
                        run_groups(plan, STEPS1[s], i, t1)
                    transpose_tile(t1, s, plan.last)
                    if not (plan.first and s == 0) and not (plan.last and s == T1_IMAGE - 1):
                        run_groups(plan, STEPS1[s], i, t1)

            image1(0)
            with pe.Fori(1, IMAGES - 1) as i:
                image1(i)
            image1(IMAGES - 1)
            pe.wait_ge(pt_split, SPLIT_CREDIT + 2 * (T1_BASE + T1_IMAGE * IMAGES))
            for side, name in enumerate(EPILOGUE_AV):
                group(plan_epilogue, name, [
                    (v_st[:, b, HEADS - 1, :, :].rearrange("p v d -> p (v d)"), src[:, 1, b, col(side, SIDE)])
                    for b in range(NT) for src in (pt_hi, pt_lo)], slice(0, SIDE))
            pe.wait_ge(o_split, FREE_CREDIT + 4 * IMAGES - 1)
            for side, name in enumerate(EPILOGUE_OUT):
                pe.wait_ge(side_split, side + 1)
                bank_free(plan_epilogue, name)
                for o in range(KT):
                    ins = run(acc[:, plan_epilogue.bank(name), col(o, SIDE)],
                              over_k(lambda part, k: wp(part, k, col(o, P)),
                                     lambda part, k: (o_hi, o_lo)[part][:, k, col(side, SIDE)]))
                ins.then_inc(acc_done, 1)


_IN = {"x": "x", "b": "L0_conv_Wb", "c": "L0_conv_Wc", "d": "L0_conv_Wd", "q": "L1_conv_wq",
       "k": "L1_conv_wk", "v": "L1_conv_wv", "p": "L1_conv_wp"}


def kernel(**inputs):
    import numpy as np
    import concourse.bacc as bacc
    from concourse.bass_utils import run_bass_kernel_spmd

    x = np.ascontiguousarray(inputs["x"])
    arrays = {
        "in_x": x.reshape(IMAGES, KT, P, N),
    }
    for w in "bc":
        arrays[f"in_w{w}"] = np.ascontiguousarray(inputs[_IN[w]])
    arrays["in_wlater"] = np.ascontiguousarray(
        np.stack([np.asarray(inputs[_IN[w]]).T for w in LATER_WEIGHTS]).reshape(-1, P, C))
    columns = [np.asarray(inputs[n]).reshape(KT, P).T for n in (
        "L1_conv_bq", "L1_conv_bk", "L1_conv_bv", "L1_conv_bp", "L1_conv_gamma", "L1_conv_beta")]
    columns.append(np.broadcast_to(np.asarray(inputs["L0_conv_gamma"]).reshape(1, 1), (P, 1)))
    arrays["in_vecs"] = np.ascontiguousarray(np.concatenate(columns, axis=1))

    nc = bacc.Bacc("TRN2", target_bir_lowering=False, num_devices=1)
    t = {n: nc.dram_tensor(n, a.shape, F32, kind="ExternalInput").ap() for n, a in arrays.items()}
    out = nc.dram_tensor("out_0", (IMAGES, KT, P, N), F32, kind="ExternalOutput").ap()
    build(nc, t["in_x"], {w: t[f"in_w{w}"] for w in ("b", "c", "later")}, t["in_vecs"], out)
    r = run_bass_kernel_spmd(nc, [arrays], core_ids=[0])
    return r.results[0]["out_0"].reshape(IMAGES, C, 32, 32)
```
